# Optimizing a Trainium2 kernel written in Bass

```python
import numpy as np
import jax
import jax.numpy as jnp

def _softmax(x, axis=-1):
    return jax.nn.softmax(x, axis=axis)

def _gelu(x):
    return jax.nn.gelu(x, approximate=True)

def _silu(x):
    return jax.nn.silu(x)

def _sigmoid(x):
    return jax.nn.sigmoid(x)

def _layernorm(x, axis=-1, eps=1e-05):
    m = jnp.mean(x, axis=axis, keepdims=True)
    v = jnp.var(x, axis=axis, keepdims=True)
    return (x - m) / jnp.sqrt(v + eps)

def _scatter_add(tgt, idx, src, axis=0):
    return tgt.at[idx].add(src)

def _segment_sum(src, seg, n):
    return jax.ops.segment_sum(src, seg, n)
kernel_name = 'mk_adj_preln_d2_adj_r2_aa0d4d'

def setup_inputs(seed: int=0):
    np.random.seed(seed)
    _w = jnp.asarray

    def _rec_inputs():
        import jax
        import jax.numpy as jnp
        _gk = jax.random.key(seed)
        x = -0.0004039 + 1 * jax.random.normal(jax.random.fold_in(_gk, 1), (128, 128, 384), jnp.float32)
        _w = (1.0 + jnp.arange(128, dtype=jnp.float32)) ** (-0.5)
        _w = _w / _w.mean()
        _pij = jnp.clip(0.0625 * _w[:, None] * _w[None, :], 0.0, 1.0)
        _a = jax.random.uniform(jax.random.fold_in(_gk, 2), (128, 128, 128)) < _pij
        _af = _a.astype(jnp.float32)
        adj = _af
        return (x, adj)
    x, adj = _rec_inputs()

    def _L0_gnn_setup():
        import jax, jax.numpy as jnp
        import numpy as np
        B, S, H, L = (32, 256, 384, 2)

        def _layer_norm(z, a, b, eps=0.001):
            mu = jnp.mean(z, axis=-1, keepdims=True)
            sigma = jnp.std(z, axis=-1, keepdims=True, ddof=1)
            return (z - mu) / (sigma + eps) * a + b
        key = jax.random.key(seed)
        ks = jax.random.split(key, 6)
        hidden_state = jax.random.normal(ks[0], (B, S, H), dtype=jnp.float32)
        adjacency_matrix = (jax.random.uniform(ks[1], (B, S, S)) < 0.2).astype(jnp.float32)
        W_left = 0.05 * jax.random.normal(ks[2], (L, H, H), dtype=jnp.float32)
        W_right = 0.05 * jax.random.normal(ks[3], (L, H, H), dtype=jnp.float32)
        W_lin = 0.05 * jax.random.normal(ks[4], (L, H, H), dtype=jnp.float32)
        b_lin = jnp.zeros((L, H), dtype=jnp.float32)
        ln_a = jnp.ones((L, H), dtype=jnp.float32)
        ln_b = jnp.zeros((L, H), dtype=jnp.float32)
        return {'hidden_state': hidden_state, 'adjacency_matrix': adjacency_matrix, 'W_left': W_left, 'W_right': W_right, 'W_lin': W_lin, 'b_lin': b_lin, 'ln_a': ln_a, 'ln_b': ln_b}
    _L0_gnn_all = _L0_gnn_setup()
    _L0_gnn_in = {k: v for k, v in _L0_gnn_all.items() if k in ('W_left', 'W_right', 'W_lin', 'b_lin', 'ln_a', 'ln_b')}
    del _L0_gnn_all

    def _L1_gnn_setup():
        import jax, jax.numpy as jnp
        import numpy as np
        B, L, H = (8, 1024, 384)
        LN_EPS = 1e-12
        key = jax.random.key(seed)
        ks = jax.random.split(key, 10)
        hidden_state = jax.random.normal(ks[0], (B, L, H), dtype=jnp.float32)
        adjacency = jax.random.randint(ks[1], (B, L, L), 0, 2).astype(jnp.float32)
        bound = 1.0 / np.sqrt(H)
        W_left = jax.random.normal(ks[2], (H, H), dtype=jnp.float32) * np.sqrt(2.0 / (H + H))
        b_left = jax.random.uniform(ks[3], (H,), minval=-bound, maxval=bound, dtype=jnp.float32)
        W_self = jax.random.normal(ks[4], (H, H), dtype=jnp.float32) * np.sqrt(2.0 / (H + H))
        b_self = jax.random.uniform(ks[5], (H,), minval=-bound, maxval=bound, dtype=jnp.float32)
        W_right = jax.random.normal(ks[6], (H, H), dtype=jnp.float32) * np.sqrt(2.0 / (H + H))
        b_right = jax.random.uniform(ks[7], (H,), minval=-bound, maxval=bound, dtype=jnp.float32)
        gamma = jnp.ones((H,), dtype=jnp.float32)
        beta = jnp.zeros((H,), dtype=jnp.float32)
        return {'hidden_state': hidden_state, 'adjacency': adjacency, 'W_left': W_left, 'b_left': b_left, 'W_self': W_self, 'b_self': b_self, 'W_right': W_right, 'b_right': b_right, 'gamma': gamma, 'beta': beta}
    _L1_gnn_all = _L1_gnn_setup()
    _L1_gnn_in = {k: v for k, v in _L1_gnn_all.items() if k in ('W_left', 'b_left', 'W_self', 'b_self', 'W_right', 'b_right', 'gamma', 'beta')}
    del _L1_gnn_all
    return {'x': x, 'adj': adj, 'L0_gnn_W_left': _L0_gnn_in['W_left'], 'L0_gnn_W_right': _L0_gnn_in['W_right'], 'L0_gnn_W_lin': _L0_gnn_in['W_lin'], 'L0_gnn_b_lin': _L0_gnn_in['b_lin'], 'L0_gnn_ln_a': _L0_gnn_in['ln_a'], 'L0_gnn_ln_b': _L0_gnn_in['ln_b'], 'L1_gnn_W_left': _L1_gnn_in['W_left'], 'L1_gnn_b_left': _L1_gnn_in['b_left'], 'L1_gnn_W_self': _L1_gnn_in['W_self'], 'L1_gnn_b_self': _L1_gnn_in['b_self'], 'L1_gnn_W_right': _L1_gnn_in['W_right'], 'L1_gnn_b_right': _L1_gnn_in['b_right'], 'L1_gnn_gamma': _L1_gnn_in['gamma'], 'L1_gnn_beta': _L1_gnn_in['beta']}

def reference(x, adj, L0_gnn_W_left, L0_gnn_W_right, L0_gnn_W_lin, L0_gnn_b_lin, L0_gnn_ln_a, L0_gnn_ln_b, L1_gnn_W_left, L1_gnn_b_left, L1_gnn_W_self, L1_gnn_b_self, L1_gnn_W_right, L1_gnn_b_right, L1_gnn_gamma, L1_gnn_beta):
    import jax
    import jax.numpy as jnp

    def _L0_gnn_ref(hidden_state, adjacency_matrix, W_left, W_right, W_lin, b_lin, ln_a, ln_b):
        import jax, jax.numpy as jnp
        import numpy as np
        B, S, H, L = (32, 256, 384, 2)

        def _layer_norm(z, a, b, eps=0.001):
            mu = jnp.mean(z, axis=-1, keepdims=True)
            sigma = jnp.std(z, axis=-1, keepdims=True, ddof=1)
            return (z - mu) / (sigma + eps) * a + b
        temper = float(np.sqrt(H))
        adj = adjacency_matrix
        adj_tri = jnp.triu(adj, k=1)
        diag_mask = jnp.triu(adj, k=0) - adj_tri
        h = hidden_state
        for l in range(L):
            m_left = jnp.einsum('bsh,oh->bso', h, W_left[l])
            m_right = jnp.einsum('bsh,oh->bso', h, W_right[l])
            u_left = jnp.einsum('bih,bjh->bij', h, m_left) / temper
            u_right = jnp.einsum('bih,bjh->bij', h, m_right) / temper
            u = u_left * adj_tri + u_left * diag_mask + u_right * jnp.swapaxes(adj_tri, 1, 2)
            delta_exp_u = jnp.exp(u) * adj
            attention = delta_exp_u / (jnp.sum(delta_exp_u, axis=2, keepdims=True) + 1e-10)
            h_lin = jnp.einsum('bsh,oh->bso', h, W_lin[l]) + b_lin[l]
            ctx = jnp.matmul(attention, h_lin)
            h = jax.nn.relu(_layer_norm(ctx, ln_a[l], ln_b[l]))
        return h

    def _L1_gnn_ref(hidden_state, adjacency, W_left, b_left, W_self, b_self, W_right, b_right, gamma, beta):
        import jax, jax.numpy as jnp
        import numpy as np
        B, L, H = (8, 1024, 384)
        LN_EPS = 1e-12
        h = hidden_state
        d = h.shape[-1]
        n = h.shape[1]
        u = jnp.einsum('bld,bmd->blm', h, h) / jnp.sqrt(jnp.asarray(d, h.dtype))
        p = jax.nn.softmax(u, axis=-1)
        delta = p * adjacency
        attn = delta / (jnp.sum(delta, axis=2, keepdims=True) + 1e-10)
        h_left = jnp.einsum('bld,ed->ble', h, W_left) + b_left
        h_self = jnp.einsum('bld,ed->ble', h, W_self) + b_self
        h_right = jnp.einsum('bld,ed->ble', h, W_right) + b_right
        i = jnp.arange(n)[:, None]
        j = jnp.arange(n)[None, :]
        attn_left = jnp.where(j > i, attn, 0.0)
        attn_right = jnp.where(j < i, attn, 0.0)
        diag_a = jnp.diagonal(attn, axis1=1, axis2=2)
        ctx = jnp.einsum('blm,bmd->bld', attn_left, h_left) + diag_a[..., None] * h_self + jnp.einsum('blm,bmd->bld', attn_right, h_right)
        mu = jnp.mean(ctx, axis=-1, keepdims=True)
        var = jnp.mean(jnp.square(ctx - mu), axis=-1, keepdims=True)
        o = (ctx - mu) / jnp.sqrt(var + LN_EPS) * gamma + beta
        return jax.nn.relu(o)
    h = jnp.maximum(_layernorm(x, axis=-1), 0.0)
    x = x + _L0_gnn_ref(h, adj, L0_gnn_W_left, L0_gnn_W_right, L0_gnn_W_lin, L0_gnn_b_lin, L0_gnn_ln_a, L0_gnn_ln_b)
    h = jnp.maximum(_layernorm(x, axis=-1), 0.0)
    x = x + _L1_gnn_ref(h, adj, L1_gnn_W_left, L1_gnn_b_left, L1_gnn_W_self, L1_gnn_b_self, L1_gnn_W_right, L1_gnn_b_right, L1_gnn_gamma, L1_gnn_beta)
    return x

_drawn_inputs = setup_inputs


def setup_inputs(seed=0):
    import zlib

    import numpy as np

    out = dict(_drawn_inputs(seed))
    spreads = {'L0_gnn_b_lin': (0.0, 0.1),
     'L0_gnn_ln_a': (1.0, 0.2),
     'L0_gnn_ln_b': (0.0, 0.1),
     'L1_gnn_gamma': (1.0, 0.2),
     'L1_gnn_beta': (0.0, 0.1)}
    factors = {'L0_gnn_W_right': 4.124,
     'L1_gnn_b_left': 4.995,
     'L1_gnn_b_self': 8.0,
     'L1_gnn_b_right': 3.07}
    for name, (base, spread) in spreads.items():
        noise = np.random.default_rng([zlib.crc32(name.encode()), seed]).standard_normal(out[name].shape)
        drawn = base * np.exp(spread * noise) if base else spread * noise
        out[name] = jnp.asarray(drawn.astype(out[name].dtype))
    for name, factor in factors.items():
        out[name] = (out[name] * factor).astype(out[name].dtype)
    return out
```

```python
from contextlib import ExitStack

import concourse.bass as bass
from concourse import mybir

F32 = mybir.dt.float32
F32R = mybir.dt.float32r
ALU = mybir.AluOpType
ACT = mybir.ActivationFunctionType
AX_X = mybir.AxisListType.X

P = 128
G = 4
A, B = 0, 1


def psum_jobs(order, banks, rounds, extra=0):
    return {job: ((extra + m) % banks, rounds + (extra + m) // banks + 1) for m, job in enumerate(order)}


def l0_phase(nc, x, adj, adj_t, w_left, w_right, w_lin_t, b_lin, ln_cols, ln_a1, ln_b1, x2):
    n_graphs, S, H = x.shape
    groups = n_graphs // G
    KC = H // P
    GS = G * S
    HV = H + 2
    LN_EPS = 1e-5
    SIGMA_EPS = 1e-3
    SUM_EPS = 1e-10
    TEMPER = float(H) ** 0.5
    UNBIAS = H / (H - 1.0)
    NUMBERS = (-0.5, 0.5, -1.0, LN_EPS, UNBIAS, SIGMA_EPS)
    RSQRT, SQRT, RECIP, N_LN_EPS, N_UNBIAS, N_SIGMA_EPS = range(6)
    assert S == P and H % P == 0

    with ExitStack() as ctx:
        def sb(name, shape, dt=F32):
            return ctx.enter_context(nc.sbuf_tensor(name, shape, dt))

        def sem(name):
            return ctx.enter_context(nc.semaphore("l0_" + name))

        def sems(name, n=2):
            return [sem(f"{name}{i}") for i in range(n)]

        w_hi = [[sb(f"w_hi{s}{w}", [P, KC, H], F32R) for w in range(3)] for s in (A, B)]
        w_lo = [[sb(f"w_lo{s}{w}", [P, KC, H], F32R) for w in range(3)] for s in (A, B)]
        bias = sb("bias", [P, 2, H])
        cols = sb("cols", [P, 2, KC])
        a1 = sb("a1", [P, H])
        b1 = sb("b1", [P, H])
        ident = sb("ident", [P, P])
        after = sb("after", [P, P])
        num = sb("num", [P, len(NUMBERS), G])

        xin = sb("xin", [P, G, H])
        xres = sb("xres", [P, G, H])
        adj_n = [sb(f"adj_n{s}", [P, G, S]) for s in (A, B)]
        adj_tr = [sb(f"adj_tr{s}", [P, G, S]) for s in (A, B)]
        m_left = [sb(f"m_left{s}", [P, G, S]) for s in (A, B)]
        m_right = [sb(f"m_right{s}", [P, G, S]) for s in (A, B)]
        ht = [sb(f"ht{s}", [P, KC, GS]) for s in (A, B)]
        ht_hi = [sb(f"ht_hi{s}", [P, KC, GS], F32R) for s in (A, B)]
        ht_lo = [sb(f"ht_lo{s}", [P, KC, GS], F32R) for s in (A, B)]
        pt_hi = sb("pt_hi", [P, KC, 2, GS], F32R)
        pt_lo = sb("pt_lo", [P, KC, 2, GS], F32R)
        val = sb("val", [P, G, H])
        val_hi = sb("val_hi", [P, G, HV], F32R)
        val_lo = sb("val_lo", [P, G, HV], F32R)
        um = sb("um", [P, 2, G, S])
        eu = sb("eu", [P, G, S])
        eu_hi = sb("eu_hi", [P, G, S], F32R)
        eu_lo = sb("eu_lo", [P, G, S], F32R)
        c = [sb(f"c{s}", [P, G, HV]) for s in (A, B)]
        rsum = [sb(f"rsum{s}", [P, 2, G]) for s in (A, B)]
        stats = [sb(f"stats{s}", [P, G, 6]) for s in (A, B, 2)]
        mv = [sb(f"mv{s}", [P, G, 2]) for s in (A, B, 2)]
        inv = [sb(f"inv{s}", [P, 4, G]) for s in (A, B, 2)]

        staging = [b[:, 0:KC, 0:H] for b in (val, c[A], xres, ht[B], c[B], xres)]

        pp = [ctx.enter_context(nc.psum_tensor(f"pp{i}", [P, 512], F32)) for i in range(3)]
        pq = [ctx.enter_context(nc.psum_tensor(f"pq{i}", [P, 512], F32)) for i in range(5)]
        p_full, p_empty = sems("p_full", 3), sems("p_empty", 3)
        q_full, q_empty = sems("q_full", 5), sems("q_empty", 5)

        ident_zero, ident_ready = sem("ident_zero"), sem("ident_ready")
        consts_loaded = sem("consts_loaded")
        consts_set = sem("consts_set")
        w_loaded, w_hi_ready, w_ready = sems("w_loaded", 6), sem("w_hi_ready"), sem("w_ready")
        x_loaded, xres_loaded, x2_stored = sem("x_loaded"), sem("xres_loaded"), sem("x2_stored")
        adj_loaded = sems("adj_loaded")
        masks_ready = sems("masks_ready")
        z_ready = sems("z_ready")
        ht_lo_ready = sems("ht_lo_ready")
        pt_hi_ready = sems("pt_hi_ready")
        val_hi_ready, val_lo_ready = sems("val_hi_ready"), sems("val_lo_ready")
        scores_summed, exp_ready = sems("scores_summed"), sems("exp_ready")
        e_ready, e_hi_ready, e_lo_ready = sems("e_ready"), sems("e_hi_ready"), sems("e_lo_ready")
        rsum_eps, rsum_ready, c_scaled = sems("rsum_eps"), sems("rsum_ready"), sems("c_scaled")
        bn_ready, mv_ready = sems("bn_ready", 3), sems("mv_ready", 3)
        inv_step, inv_ready = sems("inv_step", 3), sems("inv_ready", 3)
        fin_z, fin_a, fin_b, x2_ready = sem("fin_z"), sem("fin_a"), sem("fin_b"), sem("x2_ready")

        x_g = x.rearrange("(g b) s h -> g s b h", b=G)
        x2_g = x2.rearrange("(g b) s h -> g s b h", b=G)
        adj_g = adj.rearrange("(g b) i j -> g i b j", b=G)
        adj_t_g = adj_t.rearrange("(g b) j i -> g j b i", b=G)

        def jobs(t, a, b, n, f):
            order_p, order_q = [], []
            if a:
                order_p += [("pt", A, j) for j in range(2 * KC)]
            if f:
                order_q += [("ctx", B, i) for i in range(G)]
            if b:
                order_p += [("ht", B, k) for k in range(KC)]
            if a:
                order_q += [("val", A, 0), ("val", A, 1), ("u", A, 0), ("u", A, 1), ("val", A, 2), ("val", A, 3)]
            if b:
                order_p += [("pt", B, j) for j in range(2 * KC)]
            if a:
                order_q += [("ctx", A, i) for i in range(G)]
            if b:
                order_q += [("u", B, 0), ("u", B, 1)] + [("val", B, i) for i in range(G)]
            if n:
                order_p += [("ht", A, k) for k in range(KC)]
            if isinstance(t, int):
                n_a, n_b = min(t, groups) if t > 0 else 0, max(0, min(t - 1, groups))
                n_n, n_f = min(t + 1, groups), max(0, t - 2)
                rounds_q, extra_q = divmod(10 * n_a + 6 * n_b + 4 * n_f, 5)
                return {**psum_jobs(order_p, 3, 2 * n_a + 3 * n_b + n_n),
                        **psum_jobs(order_q, 5, rounds_q, extra_q)}
            return {**psum_jobs(order_p, 3, 6 * t - 2), **psum_jobs(order_q, 5, 4 * t - 3, 1)}

        def bank_of(job, table):
            ring = (pp, p_full, p_empty) if job[0] in ("ht", "pt") else (pq, q_full, q_empty)
            n, use = table[job]
            return ring[0][n], ring[1][n], ring[2][n], use

        def run(engine, iteration):
            def flags(t):
                return 0 <= t < groups, 1 <= t <= groups, -1 <= t < groups - 1, 2 <= t <= groups + 1
            for t in range(-1, 3):
                iteration(t, *flags(t))
            with engine.Fori(3, groups - 1) as t:
                iteration(t, True, True, True, True)
            for t in range(groups - 1, groups + 2):
                iteration(t, *flags(t))

        block = ctx.enter_context(nc.Block())

        @block.sync
        def _(sp):
            def load_x(g):
                sp.dma_start(xin[:], x_g[g]).then_inc(x_loaded, 16)

            def load_adj(s, g):
                sp.dma_start(adj_tr[s][:], adj_t_g[g]).then_inc(adj_loaded[s], 16)
                sp.dma_start(adj_n[s][:], adj_g[g]).then_inc(adj_loaded[s], 16)

            def load_weights(s, w):
                src = (w_left, w_right, w_lin_t)[w][s].rearrange("(k p) n -> p k n", p=P)
                sp.dma_start(staging[3 * s + w], src).then_inc(w_loaded[3 * s + w], 16)

            load_x(0)
            for w in range(3):
                load_weights(A, w)
            sp.dma_start(cols[:], ln_cols).then_inc(consts_loaded, 16)
            sp.dma_start(bias[:], b_lin.partition_broadcast(P)).then_inc(consts_loaded, 16)
            sp.dma_start(a1[:], ln_a1.partition_broadcast(P)).then_inc(consts_loaded, 16)
            sp.dma_start(b1[:], ln_b1.partition_broadcast(P)).then_inc(consts_loaded, 16)
            load_weights(B, 0)
            load_weights(B, 1)

            def iteration(t, a, b, n, f):
                at = isinstance(t, int)
                if n and not (at and t < 0):
                    sp.wait_ge(ht_lo_ready[A], KC * (t + 1))
                    load_x(t + 1)
                if a:
                    if not at or t >= 1:
                        sp.wait_ge(e_ready[A], t)
                    load_adj(A, t)
                    if at and t == 0:
                        sp.wait_ge(w_ready, 3)
                        load_weights(B, 2)
                if b:
                    if not at or t >= 2:
                        sp.wait_ge(e_ready[B], t - 1)
                    load_adj(B, t - 1)
                if f:
                    sp.wait_ge(x2_ready, t - 1)
                    sp.dma_start(x2_g[t - 2], xres[:]).then_inc(x2_stored, 16)
                    sp.wait_ge(x2_stored, 16 * (t - 1))
                if b:
                    if at and t == 1:
                        sp.wait_ge(w_ready, 6)
                    sp.dma_start(xres[:], x_g[t - 1]).then_inc(xres_loaded, 16)

            run(sp, iteration)

        @block.tensor
        def _(pe):
            def open_bank(job, table):
                bank, full, empty, use = bank_of(job, table)
                if not isinstance(use, int) or use > 1:
                    pe.wait_ge(empty, use - 1)
                return bank, full

            def transposes(s, table, src):
                for k in range(KC):
                    bank, full = open_bank(("ht", s, k), table)
                    for i in range(G):
                        mm = pe.transpose(bank[:, i * S:(i + 1) * S], src[:, i, k * P:(k + 1) * P], ident[:])
                    mm.then_inc(full, 1)

            def split_product(out, pairs):
                last = len(pairs) - 1
                for n, ((l_hi, l_lo), (r_hi, r_lo)) in enumerate(pairs):
                    pe.matmul(out, l_hi, r_hi, start=(n == 0), stop=False)
                    pe.matmul(out, l_hi, r_lo, start=False, stop=False)
                    mm = pe.matmul(out, l_lo, r_hi, start=False, stop=(n == last))
                return mm

            def project(s, table):
                for j in range(2 * KC):
                    m, w = j // 2, j % 2
                    bank, full = open_bank(("pt", s, j), table)
                    cut = slice(m * P, (m + 1) * P)
                    split_product(bank[:], [
                        ((w_hi[s][w][:, k, cut], w_lo[s][w][:, k, cut]), (ht_hi[s][:, k, :], ht_lo[s][:, k, :]))
                        for k in range(KC)]).then_inc(full, 1)

            def values(s, graphs, table):
                for i in graphs:
                    bank, full = open_bank(("val", s, i), table)
                    cut = slice(i * S, (i + 1) * S)
                    split_product(bank[:, 0:H], [
                        ((ht_hi[s][:, k, cut], ht_lo[s][:, k, cut]), (w_hi[s][2][:, k, :], w_lo[s][2][:, k, :]))
                        for k in range(KC)]).then_inc(full, 1)

            def scores(s, table):
                for half in range(2):
                    bank, full = open_bank(("u", s, half), table)
                    for i in (2 * half, 2 * half + 1):
                        cut = slice(i * S, (i + 1) * S)
                        at = (i % 2) * 2 * S
                        mm = split_product(bank[:, at:at + 2 * S].rearrange("p (w i) -> p w i", w=2), [
                            ((ht_hi[s][:, k, cut], ht_lo[s][:, k, cut]), (pt_hi[:, k, :, cut], pt_lo[:, k, :, cut]))
                            for k in range(KC)])
                    mm.then_inc(full, 1)

            def context(s, g, table):
                pe.wait_ge(e_lo_ready[s], g + 1)
                for i in range(G):
                    pe.wait_ge(val_lo_ready[s], G * g + i + 1)
                    bank, full = open_bank(("ctx", s, i), table)
                    split_product(bank[:, 0:HV], [
                        ((eu_hi[:, i, :], eu_lo[:, i, :]), (val_hi[:, i, :], val_lo[:, i, :]))]).then_inc(full, 1)

            pe.wait_ge(ident_ready, 1)

            def iteration(t, a, b, n, f):
                table = jobs(t, a, b, n, f)
                if isinstance(t, int) and t == 0:
                    pe.wait_ge(w_ready, 2)
                if isinstance(t, int) and t == 1:
                    pe.wait_ge(w_ready, 6)
                if a:
                    pe.wait_ge(ht_lo_ready[A], KC * (t + 1))
                    project(A, table)
                if f:
                    context(B, t - 2, table)
                if b:
                    pe.wait_ge(z_ready[B], t)
                    transposes(B, table, c[A])
                if a:
                    if isinstance(t, int) and t == 0:
                        pe.wait_ge(w_ready, 3)
                    values(A, (0, 1), table)
                    _, _, empty, use = bank_of(("pt", A, 2 * KC - 1), table)
                    pe.wait_ge(empty, use)
                    scores(A, table)
                    values(A, (2, 3), table)
                if b:
                    pe.wait_ge(ht_lo_ready[B], KC * t)
                    project(B, table)
                if a:
                    context(A, t, table)
                if b:
                    _, _, empty, use = bank_of(("pt", B, 2 * KC - 1), table)
                    pe.wait_ge(empty, use)
                    scores(B, table)
                    values(B, (0,), table)
                if n:
                    pe.wait_ge(z_ready[A], t + 2)
                    transposes(A, table, xin)
                if b:
                    values(B, (1, 2, 3), table)

            run(pe, iteration)

        @block.scalar
        def _(act):
            def turned(s, table):
                for k in range(KC):
                    bank, full, empty, use = bank_of(("ht", s, k), table)
                    act.wait_ge(full, use)
                    affine = {} if s == A else {"scale": cols[:, 0, k:k + 1], "bias": cols[:, 1, k:k + 1]}
                    act.activation(ht_hi[s][:, k, :], bank[:], ACT.Relu, **affine)
                    act.activation(ht[s][:, k, :], bank[:], ACT.Relu, **affine).then_inc(empty, 1)

            def pt_high(s, js, table):
                for j in js:
                    bank, full, _, use = bank_of(("pt", s, j), table)
                    act.wait_ge(full, use)
                    act.copy(pt_hi[:, j // 2, j % 2, :], bank[:]).then_inc(pt_hi_ready[s], 1)

            def val_high(s, graphs, table):
                for i in graphs:
                    _, _, empty, use = bank_of(("val", s, i), table)
                    act.wait_ge(empty, use)
                    act.copy(val_hi[:, i, 0:H], val[:, i, :]).then_inc(val_hi_ready[s], 1)

            def exponential(s, g):
                act.wait_ge(scores_summed[s], g + 1)
                act.activation(eu[:], eu[:], ACT.Exp, scale=1.0 / TEMPER).then_inc(exp_ready[s], 1)

            def e_high(s, g):
                act.wait_ge(e_ready[s], g + 1)
                act.copy(eu_hi[:], eu[:]).then_inc(e_hi_ready[s], 1)

            def context_out(s, table):
                for i in range(G):
                    bank, full, empty, use = bank_of(("ctx", s, i), table)
                    act.wait_ge(full, use)
                    act.copy(c[s][:, i, :], bank[:, 0:HV]).then_inc(empty, 1)

            def context_scale(s, g, table):
                _, _, empty, use = bank_of(("ctx", s, G - 1), table)
                act.wait_ge(empty, use)
                act.wait_ge(rsum_ready[s], g + 1)
                for i in range(G):
                    act.activation(c[s][:, i, 0:H], c[s][:, i, 0:H], ACT.Copy,
                                   scale=rsum[s][:, 1, i:i + 1]).then_inc(c_scaled[s], 1)

            act.wait_ge(consts_loaded, 4 * 16)

            def iteration(t, a, b, n, f):
                table = jobs(t, a, b, n, f)
                if a:
                    pt_high(A, range(2 * KC), table)
                if f:
                    if not isinstance(t, int) or t >= 3:
                        act.wait_ge(x2_ready, t - 2)
                    context_out(B, table)
                if b:
                    turned(B, table)
                if f:
                    context_scale(B, t - 2, table)
                if a:
                    val_high(A, range(G), table)
                    exponential(A, t)
                if b:
                    pt_high(B, range(0, 2), table)
                if a:
                    e_high(A, t)
                if b:
                    pt_high(B, range(2, 2 * KC), table)
                if a:
                    context_out(A, table)
                    context_scale(A, t, table)
                if b:
                    val_high(B, (0,), table)
                if n:
                    turned(A, table)
                if b:
                    exponential(B, t - 1)
                    val_high(B, (1,), table)
                    e_high(B, t - 1)
                    val_high(B, (2, 3), table)

            run(act, iteration)

        @block.vector
        def _(dve):
            def moments(s, g, src, step):
                for i in range(G):
                    if step is not None:
                        dve.wait_ge(step, G * g + i + 1)
                    bn = dve.bn_stats(stats[s][:, i, :], src[:, i, 0:H])
                bn.then_inc(bn_ready[s], 1)
                dve.wait_ge(consts_set, 1)
                dve.wait_ge(bn_ready[s], g + 1)
                for i in range(G):
                    ag = dve.bn_aggr(mv[s][:, i, :], stats[s][:, i, :])
                ag.then_inc(mv_ready[s], 1)

            def centre(s, g, src):
                dve.wait_ge(inv_ready[s], g + 1)
                for i in range(G):
                    z = dve.tensor_scalar(src[:, i, 0:H], src[:, i, 0:H], mv[s][:, i, 0:1],
                                          inv[s][:, 3, i:i + 1], ALU.subtract, ALU.mult)
                return z

            def turned_low(s, table):
                for k in range(KC):
                    _, _, empty, use = bank_of(("ht", s, k), table)
                    dve.wait_ge(empty, use)
                    dve.tensor_tensor(ht_lo[s][:, k, :], ht[s][:, k, :], ht_hi[s][:, k, :].bitcast(F32),
                                      ALU.subtract).then_inc(ht_lo_ready[s], 1)

            def pt_low(s, g, js, table):
                for j in js:
                    bank, _, empty, use = bank_of(("pt", s, j), table)
                    dve.wait_ge(pt_hi_ready[s], 2 * KC * g + j + 1)
                    dve.tensor_tensor(pt_lo[:, j // 2, j % 2, :], bank[:], pt_hi[:, j // 2, j % 2, :].bitcast(F32),
                                      ALU.subtract).then_inc(empty, 1)

            def values_out(s, graphs, table, free, free_count):
                for i in graphs:
                    bank, full, empty, use = bank_of(("val", s, i), table)
                    dve.wait_ge(full, use)
                    if free is not None:
                        dve.wait_ge(free, free_count + i)
                    dve.tensor_tensor(val[:, i, :], bank[:, 0:H], bias[:, s, :], ALU.add).then_inc(empty, 1)

            def masked(s, g, table):
                dve.wait_ge(masks_ready[s], g + 1)
                for half in range(2):
                    bank, full, empty, use = bank_of(("u", s, half), table)
                    dve.wait_ge(full, use)
                    two = slice(2 * half, 2 * half + 2)
                    u = bank[:].rearrange("p (b w i) -> p b w i", b=2, w=2)
                    dve.tensor_tensor(um[:, 0, two, :], u[:, :, 0, :], m_left[s][:, two, :], ALU.mult)
                    dve.tensor_tensor(um[:, 1, two, :], u[:, :, 1, :], m_right[s][:, two, :], ALU.mult).then_inc(empty, 1)

            def e_low(s, g):
                dve.wait_ge(e_hi_ready[s], g + 1)
                dve.tensor_tensor(eu_lo[:], eu[:], eu_hi[:].bitcast(F32), ALU.subtract).then_inc(e_lo_ready[s], 1)

            def inverse_sums(s, g, table):
                _, _, empty, use = bank_of(("ctx", s, G - 1), table)
                dve.wait_ge(empty, use)
                dve.tensor_scalar(rsum[s][:, 0, :], c[s][:, :, H], SUM_EPS, None, ALU.add).then_inc(rsum_eps[s], 1)
                dve.wait_ge(rsum_eps[s], g + 1)
                dve.reciprocal(rsum[s][:, 1, :], rsum[s][:, 0, :]).then_inc(rsum_ready[s], 1)

            for n, number in enumerate(NUMBERS):
                dve.memset(num[:, n, :], number)
            dve.memset(val_hi[:, :, H:H + 1].bitcast(F32), 1.0)
            dve.memset(val_hi[:, :, H + 1:HV].bitcast(F32), 0.0)
            dve.memset(val_lo[:, :, H:HV].bitcast(F32), 0.0).then_inc(consts_set, 1)

            def front(g):
                dve.wait_ge(x_loaded, 16 * (g + 1))
                moments(2, g, xin, None)

            def split_weights(s):
                for w in range(3):
                    n = 3 * s + w
                    dve.wait_ge(w_loaded[n], 16)
                    dve.tensor_copy(w_hi[s][w][:], staging[n]).then_inc(w_hi_ready, 1)
                    dve.wait_ge(w_hi_ready, n + 1)
                    dve.tensor_tensor(w_lo[s][w][:], staging[n], w_hi[s][w][:].bitcast(F32),
                                      ALU.subtract).then_inc(w_ready, 1)

            def iteration(t, a, b, n, f):
                table = jobs(t, a, b, n, f)
                at = isinstance(t, int)
                if at and t == 0:
                    split_weights(A)
                    split_weights(B)
                    dve.wait_ge(consts_loaded, 4 * 16)
                if a:
                    pt_low(A, t, range(0, 2), table)
                if b:
                    centre(A, t - 1, c[A]).then_inc(z_ready[B], 1)
                if a:
                    pt_low(A, t, range(2, 2 * KC), table)
                if f:
                    inverse_sums(B, t - 2, table)
                if b:
                    turned_low(B, table)
                if f:
                    moments(B, t - 2, c[B], c_scaled[B])
                free = (val_lo_ready[B], G * (t - 2) + 1) if not at or t >= 2 else (None, 0)
                if a:
                    values_out(A, (0, 1), table, *free)
                    masked(A, t, table)
                    values_out(A, (2, 3), table, *free)
                if n:
                    front(t + 1)
                if b:
                    pt_low(B, t - 1, range(0, 2), table)
                if f:
                    centre(B, t - 2, c[B]).then_inc(fin_z, 1)
                if b:
                    pt_low(B, t - 1, range(2, 3), table)
                if a:
                    e_low(A, t)
                if b:
                    pt_low(B, t - 1, range(3, 2 * KC), table)
                if n:
                    centre(2, t + 1, xin).then_inc(z_ready[A], 1)
                if a:
                    inverse_sums(A, t, table)
                    moments(A, t, c[A], c_scaled[A])
                free = (val_lo_ready[A], G * t + 1) if not at or t < groups else (val_lo_ready[A], G * (groups - 1) + 1)
                if b:
                    masked(B, t - 1, table)
                    values_out(B, (0,), table, *free)
                if n:
                    turned_low(A, table)
                if b:
                    values_out(B, (1, 2, 3), table, *free)
                    e_low(B, t - 1)
                if f:
                    dve.wait_ge(fin_b, t - 1)
                    dve.wait_ge(xres_loaded, 16 * (t - 1))
                    dve.scalar_tensor_tensor(xres[:], c[B][:, :, 0:H], 0.0, xres[:], ALU.max,
                                             ALU.add).then_inc(x2_ready, 1)
            run(dve, iteration)

        @block.gpsimd
        def _(pool):
            pool.memset(ident[:], 0.0).then_inc(ident_zero, 1)
            pool.wait_ge(ident_zero, 1)
            pool.affine_select(out=ident[:], in_=ident[:], compare_op=ALU.not_equal, fill=1.0, base=0,
                               pattern=[[-1, P]], channel_multiplier=1).then_inc(ident_ready, 1)
            pool.memset(after[:], 1.0).then_inc(ident_zero, 1)
            pool.wait_ge(ident_zero, 2)
            pool.affine_select(out=after[:], in_=after[:], compare_op=ALU.is_gt, fill=0.0, base=0,
                               pattern=[[1, P]], channel_multiplier=-1).then_inc(ident_ready, 1)
            pool.wait_ge(ident_ready, 2)
            pool.wait_ge(consts_set, 1)

            def masks(s, g):
                pool.wait_ge(adj_loaded[s], 32 * (g + 1))
                pool.tensor_tensor(m_right[s][:], adj_n[s][:], after[:, None, :].to_broadcast([P, G, S]), ALU.mult)
                pool.affine_select(out=m_left[s][:], in_=adj_tr[s][:], compare_op=ALU.is_ge, fill=0.0, base=0,
                                   pattern=[[0, G], [-1, S]], channel_multiplier=1).then_inc(masks_ready[s], 1)

            def front_inverse(g):
                pool.wait_ge(mv_ready[2], g + 1)
                pool.tensor_tensor(inv[2][:, 0, :], mv[2][:, :, 1], num[:, N_LN_EPS, :], ALU.add).then_inc(inv_step[2], 1)
                pool.wait_ge(inv_step[2], g + 1)
                pool.tensor_tensor(inv[2][:, 3, :], inv[2][:, 0, :], num[:, RSQRT, :], ALU.pow).then_inc(inv_ready[2], 1)

            def sigma_inverse(s, g):
                pool.wait_ge(mv_ready[s], g + 1)
                pool.tensor_tensor(inv[s][:, 0, :], mv[s][:, :, 1], num[:, N_UNBIAS, :], ALU.mult).then_inc(inv_step[s], 1)
                pool.wait_ge(inv_step[s], 3 * g + 1)
                pool.tensor_tensor(inv[s][:, 1, :], inv[s][:, 0, :], num[:, SQRT, :], ALU.pow).then_inc(inv_step[s], 1)
                pool.wait_ge(inv_step[s], 3 * g + 2)
                pool.tensor_tensor(inv[s][:, 2, :], inv[s][:, 1, :], num[:, N_SIGMA_EPS, :], ALU.add).then_inc(inv_step[s], 1)
                pool.wait_ge(inv_step[s], 3 * g + 3)
                pool.tensor_tensor(inv[s][:, 3, :], inv[s][:, 2, :], num[:, RECIP, :], ALU.pow).then_inc(inv_ready[s], 1)

            def values_low(s, g, graphs):
                for i in graphs:
                    pool.wait_ge(val_hi_ready[s], G * g + i + 1)
                    pool.tensor_tensor(val_lo[:, i, 0:H], val[:, i, :], val_hi[:, i, 0:H].bitcast(F32),
                                       ALU.subtract).then_inc(val_lo_ready[s], 1)

            def sum_scores(s, g, table):
                _, _, empty, use = bank_of(("u", s, 1), table)
                pool.wait_ge(empty, use)
                pool.tensor_tensor(eu[:], um[:, 0], um[:, 1], ALU.add).then_inc(scores_summed[s], 1)

            def mask_exp(s, g):
                pool.wait_ge(exp_ready[s], g + 1)
                pool.tensor_tensor(eu[:], eu[:], adj_tr[s][:], ALU.mult).then_inc(e_ready[s], 1)

            def end_affine(g):
                pool.wait_ge(fin_z, g + 1)
                pool.tensor_tensor(c[B][:, :, 0:H], c[B][:, :, 0:H], a1[:, None, :].to_broadcast([P, G, H]),
                                   ALU.mult).then_inc(fin_a, 1)
                pool.wait_ge(fin_a, g + 1)
                pool.tensor_tensor(c[B][:, :, 0:H], c[B][:, :, 0:H], b1[:, None, :].to_broadcast([P, G, H]),
                                   ALU.add).then_inc(fin_b, 1)

            def iteration(t, a, b, n, f):
                table = jobs(t, a, b, n, f)
                if a:
                    masks(A, t)
                if b:
                    masks(B, t - 1)
                if a:
                    values_low(A, t, (0, 1))
                    sum_scores(A, t, table)
                if f:
                    sigma_inverse(B, t - 2)
                if a:
                    values_low(A, t, (2, 3))
                    mask_exp(A, t)
                if n:
                    front_inverse(t + 1)
                if f:
                    end_affine(t - 2)
                if b:
                    sum_scores(B, t - 1, table)
                    values_low(B, t - 1, (0,))
                    mask_exp(B, t - 1)
                    values_low(B, t - 1, (1, 2, 3))
                if a:
                    sigma_inverse(A, t)

            run(pool, iteration)


def l1_phase(nc, x2, adj_t, w_left_t, w_self_t, w_right_t, biases, gamma, beta, out):
    n_graphs, S, H = x2.shape
    groups = n_graphs // G
    KC = H // P
    GS = G * S
    HV = H + 2
    FRONT_EPS = 1e-5
    LN_EPS = 1e-12
    SUM_EPS = 1e-10
    SCALE = 1.0 / float(H) ** 0.5
    NUMBERS = (-0.5, -1.0, FRONT_EPS, LN_EPS)
    RSQRT, NEGATE, N_FRONT_EPS, N_LN_EPS = range(4)
    FRONT, END = 0, 1
    LEFT, RIGHT, SELF = 0, 1, 2

    with ExitStack() as ctx:
        def sb(name, shape, dt=F32):
            return ctx.enter_context(nc.sbuf_tensor("l1_" + name, shape, dt))

        def sem(name):
            return ctx.enter_context(nc.semaphore("l1_" + name))

        def sems(name, n=2):
            return [sem(f"{name}{i}") for i in range(n)]

        w_hi = [sb(f"w_hi{w}", [P, KC, H], F32R) for w in range(3)]
        w_lo = [sb(f"w_lo{w}", [P, KC, H], F32R) for w in range(3)]
        bias = sb("bias", [P, 3, H])
        gam = sb("gam", [P, H])
        bet = sb("bet", [P, H])
        ident = sb("ident", [P, P])
        num = sb("num", [P, len(NUMBERS), G])
        xin = sb("xin", [P, G, H])
        xres = sb("xres", [P, G, H])
        adj_tr = sb("adj_tr", [P, G, S])
        m_lr = sb("m_lr", [P, 2, G, S])
        m_self = sb("m_self", [P, G, S])
        ht = sb("ht", [P, KC, GS])
        ht_hi = sb("ht_hi", [P, KC, GS], F32R)
        ht_lo = sb("ht_lo", [P, KC, GS], F32R)
        val = [sb(f"val{w}", [P, G, H]) for w in (LEFT, RIGHT)]
        val_hi = [sb(f"val_hi{w}", [P, G, HV], F32R) for w in (LEFT, RIGHT)]
        val_lo = [sb(f"val_lo{w}", [P, G, HV], F32R) for w in (LEFT, RIGHT)]
        own = sb("own", [P, G, HV])
        neg_max = sb("neg_max", [P, 2, G])
        e = sb("e", [P, G, S])
        e_diag = sb("e_diag", [P, G, S])
        z_sum = sb("z_sum", [P, G])
        diag = sb("diag", [P, G])
        et = sb("et", [P, 2, G, S])
        et_hi = sb("et_hi", [P, 2, G, S], F32R)
        et_lo = sb("et_lo", [P, 2, G, S], F32R)
        c = sb("c", [P, G, HV])
        zc = sb("zc", [P, G, H])
        q = sb("q", [P, 4, G])
        stats = [sb(f"stats{n}", [P, G, 6]) for n in (FRONT, END)]
        mv = [sb(f"mv{n}", [P, G, 2]) for n in (FRONT, END)]
        inv = [sb(f"inv{n}", [P, 4, G]) for n in (FRONT, END)]

        pp = [ctx.enter_context(nc.psum_tensor(f"l1_pp{i}", [P, 512], F32)) for i in range(3)]
        pq = [ctx.enter_context(nc.psum_tensor(f"l1_pq{i}", [P, 512], F32)) for i in range(4)]
        p_full, p_empty = sems("p_full", 3), sems("p_empty", 3)
        q_full, q_empty = sems("q_full", 4), sems("q_empty", 4)

        ident_zero, ident_ready = sem("ident_zero"), sem("ident_ready")
        consts_loaded, consts_set = sem("consts_loaded"), sem("consts_set")
        w_loaded, w_hi_ready, w_ready = sems("w_loaded"), sem("w_hi_ready"), sem("w_ready")
        x_loaded, xres_loaded, adj_loaded = sem("x_loaded"), sem("xres_loaded"), sem("adj_loaded")
        masks_ready = sem("masks_ready")
        bn_ready, mv_ready = sems("bn_ready"), sems("mv_ready")
        inv_step, inv_ready = sems("inv_step"), sems("inv_ready")
        z_ready, ht_lo_ready = sems("z_ready"), sem("ht_lo_ready")
        max_ready, bias_ready = sem("max_ready"), sem("bias_ready")
        diag_masked, diag_ready = sem("diag_masked"), sem("diag_ready")
        et_hi_ready, et_lo_ready = sem("et_hi_ready"), sem("et_lo_ready")
        val_hi_ready, val_lo_ready = sem("val_hi_ready"), sem("val_lo_ready")
        q_ready = sem("q_ready")
        scaled, shifted, out_ready, out_stored = sem("scaled"), sem("shifted"), sem("out_ready"), sem("out_stored")

        x_g = x2.rearrange("(g b) s h -> g s b h", b=G)
        out_g = out.rearrange("(g b) s h -> g s b h", b=G)
        adj_t_g = adj_t.rearrange("(g b) j i -> g j b i", b=G)

        def jobs(t, a, n):
            order_p, order_q = [], []
            if a:
                order_p += [("u", 0), ("et", 0)]
                order_q += [("val", w, i) for w in (LEFT, RIGHT, SELF) for i in range(G)]
            if n:
                order_p += [("ht", k) for k in range(KC)]
            if a:
                order_p += [("ctx", i) for i in range(G)]
            if isinstance(t, int) and t < 0:
                return psum_jobs(order_p, 3, 0)
            return {**psum_jobs(order_p, 3, 3 * t + 1), **psum_jobs(order_q, 4, 3 * t)}

        def bank_of(job, table):
            ring = (pq, q_full, q_empty) if job[0] == "val" else (pp, p_full, p_empty)
            n, use = table[job]
            return ring[0][n], ring[1][n], ring[2][n], use

        def run(engine, iteration):
            iteration(-1, False, True, False, False)
            iteration(0, True, True, False, False)
            iteration(1, True, True, True, False)
            iteration(2, True, True, True, True)
            with engine.Fori(3, groups - 1) as t:
                iteration(t, True, True, True, True)
            iteration(groups - 1, True, False, True, True)
            iteration(groups, False, False, True, True)
            iteration(groups + 1, False, False, False, True)

        block = ctx.enter_context(nc.Block())

        @block.sync
        def _(sp):
            sp.dma_start(xin[:], x_g[0]).then_inc(x_loaded, 16)
            sp.dma_start(bias[:], biases.partition_broadcast(P)).then_inc(consts_loaded, 16)
            sp.dma_start(gam[:], gamma.partition_broadcast(P)).then_inc(consts_loaded, 16)
            sp.dma_start(bet[:], beta.partition_broadcast(P)).then_inc(consts_loaded, 16)
            for w, src in enumerate((w_left_t, w_right_t, w_self_t)):
                if w == 2:
                    sp.wait_ge(w_ready, 1)
                sp.dma_start((val[0], val[1])[w % 2][:, 0:KC, :],
                             src.rearrange("(k p) n -> p k n", p=P)).then_inc(w_loaded[w % 2], 16)

            def iteration(t, a, n, f, e_):
                if n and not (isinstance(t, int) and t < 0):
                    sp.wait_ge(ht_lo_ready, KC * (t + 1))
                    sp.dma_start(xin[:], x_g[t + 1]).then_inc(x_loaded, 16)
                if a:
                    if not isinstance(t, int) or t >= 1:
                        sp.wait_ge(masks_ready, t)
                    sp.dma_start(adj_tr[:], adj_t_g[t]).then_inc(adj_loaded, 16)
                if e_:
                    sp.wait_ge(out_ready, t - 1)
                    sp.dma_start(out_g[t - 2], xres[:]).then_inc(out_stored, 16)
                    sp.wait_ge(out_stored, 16 * (t - 1))
                if f:
                    sp.dma_start(xres[:], x_g[t - 1]).then_inc(xres_loaded, 16)

            run(sp, iteration)

        @block.tensor
        def _(pe):
            def open_bank(job, table):
                bank, full, empty, use = bank_of(job, table)
                if not isinstance(use, int) or use > 1:
                    pe.wait_ge(empty, use - 1)
                return bank, full

            def split_product(out_ap, pairs):
                last = len(pairs) - 1
                for n, ((l_hi, l_lo), (r_hi, r_lo)) in enumerate(pairs):
                    pe.matmul(out_ap, l_hi, r_hi, start=(n == 0), stop=False)
                    pe.matmul(out_ap, l_hi, r_lo, start=False, stop=False)
                    mm = pe.matmul(out_ap, l_lo, r_hi, start=False, stop=(n == last))
                return mm

            def scores(table):
                bank, full = open_bank(("u", 0), table)
                for i in range(G):
                    cut = slice(i * S, (i + 1) * S)
                    for k in range(KC):
                        mm = pe.matmul(bank[:, cut], ht[:, k, cut], ht[:, k, cut], start=(k == 0), stop=(k == KC - 1))
                mm.then_inc(full, 1)

            def values(w, table):
                for i in range(G):
                    bank, full = open_bank(("val", w, i), table)
                    cut = slice(i * S, (i + 1) * S)
                    split_product(bank[:, 0:H], [
                        ((ht_hi[:, k, cut], ht_lo[:, k, cut]), (w_hi[w][:, k, :], w_lo[w][:, k, :]))
                        for k in range(KC)]).then_inc(full, 1)

            pe.wait_ge(ident_ready, 1)

            def iteration(t, a, n, f, e_):
                table = jobs(t, a, n)
                if a:
                    pe.wait_ge(ht_lo_ready, KC * (t + 1))
                    scores(table)
                    if isinstance(t, int) and t == 0:
                        pe.wait_ge(w_ready, 3)
                    values(LEFT, table)
                    bank, full = open_bank(("et", 0), table)
                    _, _, scores_empty, use = bank_of(("u", 0), table)
                    pe.wait_ge(scores_empty, use)
                    for i in range(G):
                        mm = pe.transpose(bank[:, i * S:(i + 1) * S], e[:, i, :], ident[:])
                    mm.then_inc(full, 1)
                    values(RIGHT, table)
                    values(SELF, table)
                if n:
                    pe.wait_ge(z_ready[FRONT], t + 2)
                    for k in range(KC):
                        bank, full = open_bank(("ht", k), table)
                        for i in range(G):
                            mm = pe.transpose(bank[:, i * S:(i + 1) * S], xin[:, i, k * P:(k + 1) * P], ident[:])
                        mm.then_inc(full, 1)
                if a:
                    pe.wait_ge(et_lo_ready, t + 1)
                    pe.wait_ge(val_lo_ready, 2 * G * (t + 1))
                    for i in range(G):
                        bank, full = open_bank(("ctx", i), table)
                        split_product(bank[:, 0:HV], [
                            ((et_hi[:, w, i, :], et_lo[:, w, i, :]), (val_hi[w][:, i, :], val_lo[w][:, i, :]))
                            for w in (LEFT, RIGHT)]).then_inc(full, 1)

            run(pe, iteration)

        @block.scalar
        def _(act):
            def values_high(w, t, table):
                for i in range(G):
                    _, _, empty, use = bank_of(("val", w, i), table)
                    act.wait_ge(empty, use)
                    act.copy(val_hi[w][:, i, 0:H], val[w][:, i, :]).then_inc(val_hi_ready, 1)

            def centre(n, g, buf, z_buf):
                act.wait_ge(inv_ready[n], g + 1)
                for i in range(G):
                    z = act.activation(z_buf[:, i, 0:H], buf[:, i, 0:H], ACT.Identity, scale=inv[n][:, 3, i:i + 1],
                                       bias=inv[n][:, 2, i:i + 1])
                z.then_inc(z_ready[n], 1)

            def iteration(t, a, n, f, e_):
                table = jobs(t, a, n)
                if a:
                    bank, full, empty, use = bank_of(("u", 0), table)
                    act.wait_ge(bias_ready, t + 1)
                    for i in range(G):
                        ex = act.activation(e[:, i, :], bank[:, i * S:(i + 1) * S], ACT.Exp, scale=SCALE,
                                            bias=neg_max[:, 1, i:i + 1], accum_out=z_sum[:, i:i + 1])
                    ex.then_inc(empty, 1)
                    values_high(LEFT, t, table)
                if f:
                    if not isinstance(t, int) or t >= 2:
                        act.wait_ge(out_ready, t - 1)
                    centre(END, t - 1, c, zc)
                if a:
                    _, _, empty, use = bank_of(("et", 0), table)
                    act.wait_ge(empty, use)
                    act.copy(et_hi[:], et[:]).then_inc(et_hi_ready, 1)
                    values_high(RIGHT, t, table)
                if n:
                    centre(FRONT, t + 1, xin, xin)
                    for k in range(KC):
                        bank, full, empty, use = bank_of(("ht", k), table)
                        act.wait_ge(full, use)
                        act.activation(ht_hi[:, k, :], bank[:], ACT.Relu)
                        act.activation(ht[:, k, :], bank[:], ACT.Relu).then_inc(empty, 1)

            run(act, iteration)

        @block.vector
        def _(dve):
            def moments(n, g, src):
                for i in range(G):
                    bn = dve.bn_stats(stats[n][:, i, :], src[:, i, 0:H])
                bn.then_inc(bn_ready[n], 1)
                dve.wait_ge(consts_set, 1)
                dve.wait_ge(bn_ready[n], g + 1)
                for i in range(G):
                    ag = dve.bn_aggr(mv[n][:, i, :], stats[n][:, i, :])
                ag.then_inc(mv_ready[n], 1)

            def values_out(w, t, table):
                for i in range(G):
                    bank, full, empty, use = bank_of(("val", w, i), table)
                    dve.wait_ge(full, use)
                    if w == SELF:
                        dve.tensor_tensor(own[:, i, 0:H], bank[:, 0:H], bias[:, w, :], ALU.add).then_inc(empty, 1)
                    else:
                        dve.tensor_tensor(val[w][:, i, :], bank[:, 0:H], bias[:, w, :], ALU.add).then_inc(empty, 1)

            for n, number in enumerate(NUMBERS):
                dve.memset(num[:, n, :], number)
            dve.memset(own[:, :, H:HV], 1.0)
            for w in (LEFT, RIGHT):
                dve.memset(val_hi[w][:, :, H:H + 1].bitcast(F32), 1.0)
                dve.memset(val_hi[w][:, :, H + 1:HV].bitcast(F32), 0.0)
                last = dve.memset(val_lo[w][:, :, H:HV].bitcast(F32), 0.0)
            last.then_inc(consts_set, 1)

            def iteration(t, a, n, f, e_):
                table = jobs(t, a, n)
                if isinstance(t, int) and t == 0:
                    for w in range(3):
                        staging = val[w % 2]
                        dve.wait_ge(w_loaded[w % 2], 16 * (w // 2 + 1))
                        dve.tensor_copy(w_hi[w][:], staging[:, 0:KC, :]).then_inc(w_hi_ready, 1)
                        dve.wait_ge(w_hi_ready, w + 1)
                        dve.tensor_tensor(w_lo[w][:], staging[:, 0:KC, :], w_hi[w][:].bitcast(F32),
                                          ALU.subtract).then_inc(w_ready, 1)
                    dve.wait_ge(consts_loaded, 3 * 16)
                if a:
                    bank, full, _, use = bank_of(("u", 0), table)
                    dve.wait_ge(full, use)
                    dve.tensor_reduce(neg_max[:, 0, :], bank[:].rearrange("p (b j) -> p b j", b=G), AX_X, ALU.max,
                                      negate=True).then_inc(max_ready, 1)
                    dve.wait_ge(max_ready, t + 1)
                    dve.tensor_scalar(neg_max[:, 1, :], neg_max[:, 0, :], SCALE, None, ALU.mult).then_inc(bias_ready, 1)
                if e_:
                    dve.wait_ge(shifted, t - 1)
                    dve.wait_ge(xres_loaded, 16 * (t - 1))
                    dve.scalar_tensor_tensor(xres[:], zc[:], 0.0, xres[:], ALU.max, ALU.add).then_inc(out_ready, 1)
                if f:
                    moments(END, t - 1, c)
                if a:
                    values_out(LEFT, t, table)
                if n:
                    dve.wait_ge(x_loaded, 16 * (t + 2))
                    moments(FRONT, t + 1, xin)
                if a:
                    bank, full, empty, use = bank_of(("et", 0), table)
                    dve.wait_ge(full, use)
                    dve.wait_ge(masks_ready, t + 1)
                    turned = bank[:].rearrange("p (b i) -> p b i", b=G)
                    dve.tensor_tensor(et[:, LEFT], turned, m_lr[:, LEFT], ALU.mult)
                    dve.tensor_tensor(et[:, RIGHT], turned, m_lr[:, RIGHT], ALU.mult).then_inc(empty, 1)
                    dve.wait_ge(diag_masked, t + 1)
                    dve.tensor_reduce(diag[:], e_diag[:], AX_X, ALU.add).then_inc(diag_ready, 1)
                    values_out(RIGHT, t, table)
                    dve.wait_ge(et_hi_ready, t + 1)
                    dve.tensor_tensor(et_lo[:], et[:], et_hi[:].bitcast(F32), ALU.subtract).then_inc(et_lo_ready, 1)
                if a:
                    values_out(SELF, t, table)
                if n:
                    for k in range(KC):
                        _, _, empty, use = bank_of(("ht", k), table)
                        dve.wait_ge(empty, use)
                        dve.tensor_tensor(ht_lo[:, k, :], ht[:, k, :], ht_hi[:, k, :].bitcast(F32),
                                          ALU.subtract).then_inc(ht_lo_ready, 1)
                if a:
                    if not isinstance(t, int) or t >= 1:
                        dve.wait_ge(z_ready[END], t)
                    dve.wait_ge(diag_ready, t + 1)
                    _, _, own_landed, own_use = bank_of(("val", SELF, G - 1), table)
                    dve.wait_ge(own_landed, own_use)
                    for i in range(G):
                        bank, full, empty, use = bank_of(("ctx", i), table)
                        dve.wait_ge(full, use)
                        dve.scalar_tensor_tensor(c[:, i, 0:H + 1], own[:, i, 0:H + 1], diag[:, i:i + 1],
                                                 bank[:, 0:H + 1], ALU.mult, ALU.add).then_inc(empty, 1)
                    dve.wait_ge(empty, use)
                    dve.scalar_tensor_tensor(q[:, 0, :], z_sum[:], SUM_EPS, c[:, :, H], ALU.mult,
                                             ALU.add).then_inc(q_ready, 1)

            run(dve, iteration)

        @block.gpsimd
        def _(pool):
            pool.memset(ident[:], 0.0).then_inc(ident_zero, 1)
            pool.wait_ge(ident_zero, 1)
            pool.affine_select(out=ident[:], in_=ident[:], compare_op=ALU.not_equal, fill=1.0, base=0,
                               pattern=[[-1, P]], channel_multiplier=1).then_inc(ident_ready, 1)
            pool.wait_ge(ident_ready, 1)
            pool.wait_ge(consts_set, 1)
            pool.wait_ge(consts_loaded, 3 * 16)

            def inverse(n, step0):
                pool.tensor_tensor(inv[n][:, 3, :], inv[n][:, 0, :], num[:, RSQRT, :], ALU.pow).then_inc(inv_step[n], 1)
                pool.wait_ge(inv_step[n], step0 + 1)
                pool.tensor_tensor(inv[n][:, 1, :], inv[n][:, 3, :], mv[n][:, :, 0], ALU.mult).then_inc(inv_step[n], 1)
                pool.wait_ge(inv_step[n], step0 + 2)
                pool.tensor_tensor(inv[n][:, 2, :], inv[n][:, 1, :], num[:, NEGATE, :], ALU.mult).then_inc(inv_ready[n], 1)

            def front_inverse(g):
                pool.wait_ge(mv_ready[FRONT], g + 1)
                pool.tensor_tensor(inv[FRONT][:, 0, :], mv[FRONT][:, :, 1], num[:, N_FRONT_EPS, :],
                                   ALU.add).then_inc(inv_step[FRONT], 1)
                pool.wait_ge(inv_step[FRONT], 3 * g + 1)
                inverse(FRONT, 3 * g + 1)

            def end_inverse(g):
                pool.wait_ge(mv_ready[END], g + 1)
                pool.wait_ge(q_ready, g + 1)
                pool.tensor_tensor(q[:, 1, :], q[:, 0, :], q[:, 0, :], ALU.mult).then_inc(inv_step[END], 1)
                pool.wait_ge(inv_step[END], 5 * g + 1)
                pool.tensor_tensor(q[:, 2, :], q[:, 1, :], num[:, N_LN_EPS, :], ALU.mult).then_inc(inv_step[END], 1)
                pool.wait_ge(inv_step[END], 5 * g + 2)
                pool.tensor_tensor(inv[END][:, 0, :], q[:, 2, :], mv[END][:, :, 1], ALU.add).then_inc(inv_step[END], 1)
                pool.wait_ge(inv_step[END], 5 * g + 3)
                inverse(END, 5 * g + 3)

            def values_low(w, t):
                for i in range(G):
                    pool.wait_ge(val_hi_ready, 2 * G * t + G * w + i + 1)
                    pool.tensor_tensor(val_lo[w][:, i, 0:H], val[w][:, i, :], val_hi[w][:, i, 0:H].bitcast(F32),
                                       ALU.subtract).then_inc(val_lo_ready, 1)

            def iteration(t, a, n, f, e_):
                table = jobs(t, a, n)
                if a:
                    pool.wait_ge(adj_loaded, 16 * (t + 1))
                    pool.tensor_tensor(m_self[:], adj_tr[:], ident[:, None, :].to_broadcast([P, G, S]), ALU.mult)
                    for w, sign in ((LEFT, 1), (RIGHT, -1)):
                        sel = pool.affine_select(out=m_lr[:, w], in_=adj_tr[:], compare_op=ALU.is_gt, fill=0.0,
                                                 base=0, pattern=[[0, G], [-sign, S]], channel_multiplier=sign)
                    sel.then_inc(masks_ready, 1)
                if f:
                    end_inverse(t - 1)
                if a:
                    _, _, empty, use = bank_of(("u", 0), table)
                    pool.wait_ge(empty, use)
                    pool.wait_ge(masks_ready, t + 1)
                    pool.tensor_tensor(e_diag[:], e[:], m_self[:], ALU.mult).then_inc(diag_masked, 1)
                    values_low(LEFT, t)
                if n:
                    front_inverse(t + 1)
                if a:
                    values_low(RIGHT, t)
                if f:
                    pool.wait_ge(z_ready[END], t)
                    pool.tensor_tensor(zc[:], zc[:], gam[:, None, :].to_broadcast([P, G, H]),
                                       ALU.mult).then_inc(scaled, 1)
                    pool.wait_ge(scaled, t)
                    pool.tensor_tensor(zc[:], zc[:], bet[:, None, :].to_broadcast([P, G, H]),
                                       ALU.add).then_inc(shifted, 1)

            run(pool, iteration)


def build(nc, x, adj, adj_t, l0_w_left, l0_w_right, l0_w_lin_t, l0_b_lin, l0_ln_cols, l0_ln_a1, l0_ln_b1,
          l1_w_left_t, l1_w_self_t, l1_w_right_t, l1_biases, l1_gamma, l1_beta, out):
    x2 = nc.dram_tensor("x2_scratch", list(x.shape), F32, kind="Internal").ap()
    l0_phase(nc, x, adj, adj_t, l0_w_left, l0_w_right, l0_w_lin_t, l0_b_lin, l0_ln_cols, l0_ln_a1, l0_ln_b1, x2)
    l1_phase(nc, x2, adj_t, l1_w_left_t, l1_w_self_t, l1_w_right_t, l1_biases, l1_gamma, l1_beta, out)


def kernel(**inputs):
    import numpy as np
    import concourse.bacc as bacc
    from concourse.bass_utils import run_bass_kernel_spmd

    i = {k: np.asarray(v) for k, v in inputs.items()}
    chunks = i["x"].shape[2] // P
    laid = {
        "x": i["x"],
        "adj": i["adj"],
        "adj_t": i["adj"].transpose(0, 2, 1),
        "l0_w_left": i["L0_gnn_W_left"],
        "l0_w_right": i["L0_gnn_W_right"],
        "l0_w_lin_t": i["L0_gnn_W_lin"].transpose(0, 2, 1),
        "l0_b_lin": i["L0_gnn_b_lin"],
        "l0_ln_cols": np.stack([i["L0_gnn_ln_a"][0].reshape(chunks, P).T, i["L0_gnn_ln_b"][0].reshape(chunks, P).T], 1),
        "l0_ln_a1": i["L0_gnn_ln_a"][1],
        "l0_ln_b1": i["L0_gnn_ln_b"][1],
        "l1_w_left_t": i["L1_gnn_W_left"].T,
        "l1_w_self_t": i["L1_gnn_W_self"].T,
        "l1_w_right_t": i["L1_gnn_W_right"].T,
        "l1_biases": np.stack([i["L1_gnn_b_left"], i["L1_gnn_b_right"], i["L1_gnn_b_self"]]),
        "l1_gamma": i["L1_gnn_gamma"],
        "l1_beta": i["L1_gnn_beta"],
    }
    nc = bacc.Bacc("TRN2", target_bir_lowering=False, num_devices=1)
    arrays, args = {}, []
    for name, a in laid.items():
        a = np.ascontiguousarray(a)
        arrays[f"in_{name}"] = a
        args.append(nc.dram_tensor(f"in_{name}", a.shape, mybir.dt.from_np(a.dtype), kind="ExternalInput").ap())
    args.append(nc.dram_tensor("out_0", i["x"].shape, mybir.dt.from_np(i["x"].dtype), kind="ExternalOutput").ap())
    build(nc, *args)
    r = run_bass_kernel_spmd(nc, [arrays], core_ids=[0])
    return r.results[0]["out_0"]
```

```python
from contextlib import ExitStack

import concourse.bass as bass
from concourse import mybir

F32 = mybir.dt.float32
F32R = mybir.dt.float32r
ALU = mybir.AluOpType
ACT = mybir.ActivationFunctionType
AX_X = mybir.AxisListType.X

P = 128
G = 4
A, B = 0, 1
LN_EPS = 1e-5
L0_EPS = 1e-3
L1_EPS = 1e-12
RSQRT, SQRT, RECIP, N_LN_EPS, N_UNBIAS, N_L0_EPS, N_L1_EPS = range(7)


def psum_jobs(order, banks, rounds, extra=0):
    return {job: ((extra + m) % banks, rounds + (extra + m) // banks + 1) for m, job in enumerate(order)}


def l0_phase(nc, kept, x, adj, adj_t, w_left, w_right, w_lin_t, b_lin, ln_cols, ln_a1, ln_b1, l1_consts, l1_weights, x2):
    n_graphs, S, H = x.shape
    groups = n_graphs // G
    KC = H // P
    GS = G * S
    HV = H + 2
    SUM_EPS = 1e-10
    TEMPER = float(H) ** 0.5
    NUMBERS = (-0.5, 0.5, -1.0, LN_EPS, H / (H - 1.0), L0_EPS, L1_EPS)
    assert S == P and H % P == 0

    with ExitStack() as ctx:
        def sb(name, shape, dt=F32):
            return ctx.enter_context(nc.sbuf_tensor(name, shape, dt))

        def sem(name):
            return ctx.enter_context(nc.semaphore("l0_" + name))

        def sems(name, n=2):
            return [sem(f"{name}{i}") for i in range(n)]

        w_hi = [kept["w_hi"], [sb(f"w_hi{w}", [P, KC, H], F32R) for w in range(3)]]
        w_lo = [kept["w_lo"], [sb(f"w_lo{w}", [P, KC, H], F32R) for w in range(3)]]
        bias = sb("bias", [P, 2, H])
        cols = sb("cols", [P, 2, KC])
        a1, b1 = kept["a1"], kept["b1"]
        ident = kept["ident"]
        after = sb("after", [P, P])
        num = kept["num"]

        xin = kept["xin"]
        xres = kept["xres"]
        adj_n = [sb(f"adj_n{s}", [P, G, S]) for s in (A, B)]
        adj_tr = [sb(f"adj_tr{s}", [P, G, S]) for s in (A, B)]
        m_left = [sb(f"m_left{s}", [P, G, S]) for s in (A, B)]
        m_right = [sb(f"m_right{s}", [P, G, S]) for s in (A, B)]
        ht = [kept["ht"], sb("ht_b", [P, KC, GS])]
        ht_hi = [kept["ht_hi"], sb("ht_hi_b", [P, KC, GS], F32R)]
        ht_lo = [kept["ht_lo"], sb("ht_lo_b", [P, KC, GS], F32R)]
        pt_hi = sb("pt_hi", [P, KC, 2, GS], F32R)
        pt_lo = sb("pt_lo", [P, KC, 2, GS], F32R)
        val = sb("val", [P, G, H])
        val_hi = sb("val_hi", [P, G, HV], F32R)
        val_lo = sb("val_lo", [P, G, HV], F32R)
        um = sb("um", [P, 2, G, S])
        eu = sb("eu", [P, G, S])
        eu_hi = sb("eu_hi", [P, G, S], F32R)
        eu_lo = sb("eu_lo", [P, G, S], F32R)
        c = [sb("c_a", [P, G, HV]), kept["c"]]
        rsum = [sb(f"rsum{s}", [P, 2, G]) for s in (A, B)]
        stats = [sb(f"stats{s}", [P, G, 6]) for s in (A, B, 2)]
        mv = [sb(f"mv{s}", [P, G, 2]) for s in (A, B, 2)]
        inv = [sb(f"inv{s}", [P, 4, G]) for s in (A, B, 2)]

        staging = [b[:, 0:KC, 0:H] for b in (val, c[A], xres, ht[B], c[B], xres)]
        l1_staging = [b[:, 0:KC, 0:H] for b in (xin, c[A], xin)]

        pp = [ctx.enter_context(nc.psum_tensor(f"pp{i}", [P, 512], F32)) for i in range(3)]
        pq = [ctx.enter_context(nc.psum_tensor(f"pq{i}", [P, 512], F32)) for i in range(5)]
        p_full, p_empty = sems("p_full", 3), sems("p_empty", 3)
        q_full, q_empty = sems("q_full", 5), sems("q_empty", 5)

        ident_zero, ident_ready = sem("ident_zero"), sem("ident_ready")
        consts_loaded = sem("consts_loaded")
        consts_set = sem("consts_set")
        w_loaded, w_hi_ready, w_ready = sems("w_loaded", 9), sem("w_hi_ready"), sem("w_ready")
        l1_consts_loaded = sem("l1_consts_loaded")
        x_loaded, xres_loaded, x2_stored = sem("x_loaded"), sem("xres_loaded"), sem("x2_stored")
        adj_loaded = sems("adj_loaded")
        masks_ready = sems("masks_ready")
        z_ready = sems("z_ready")
        ht_lo_ready = sems("ht_lo_ready")
        pt_hi_ready = sems("pt_hi_ready")
        val_hi_ready, val_lo_ready = sems("val_hi_ready"), sems("val_lo_ready")
        scores_summed, exp_ready = sems("scores_summed"), sems("exp_ready")
        e_ready, e_hi_ready, e_lo_ready = sems("e_ready"), sems("e_hi_ready"), sems("e_lo_ready")
        rsum_eps, rsum_ready, c_scaled = sems("rsum_eps"), sems("rsum_ready"), sems("c_scaled")
        bn_ready, mv_ready = sems("bn_ready", 3), sems("mv_ready", 3)
        inv_step, inv_ready = sems("inv_step", 3), sems("inv_ready", 3)
        fin_z, fin_a, fin_b, x2_ready = sem("fin_z"), sem("fin_a"), sem("fin_b"), sem("x2_ready")

        x_g = x.rearrange("(g b) s h -> g s b h", b=G)
        x2_g = x2.rearrange("(g b) s h -> g s b h", b=G)
        adj_g = adj.rearrange("(g b) i j -> g i b j", b=G)
        adj_t_g = adj_t.rearrange("(g b) j i -> g j b i", b=G)

        def jobs(t, a, b, n, f):
            order_p, order_q = [], []
            if a:
                order_p += [("pt", A, j) for j in range(2 * KC)]
            if f:
                order_q += [("ctx", B, i) for i in range(G)]
            if b:
                order_p += [("ht", B, k) for k in range(KC)]
            if a:
                order_q += [("val", A, 0), ("val", A, 1), ("u", A, 0), ("u", A, 1), ("val", A, 2), ("val", A, 3)]
            if b:
                order_p += [("pt", B, j) for j in range(2 * KC)]
            if a:
                order_q += [("ctx", A, i) for i in range(G)]
            if b:
                order_q += [("u", B, 0), ("u", B, 1)] + [("val", B, i) for i in range(G)]
            if n:
                order_p += [("ht", A, k) for k in range(KC)]
            if isinstance(t, int):
                n_a, n_b = min(t, groups) if t > 0 else 0, max(0, min(t - 1, groups))
                n_n, n_f = min(t + 1, groups + 1), max(0, t - 2)
                rounds_q, extra_q = divmod(10 * n_a + 6 * n_b + 4 * n_f, 5)
                return {**psum_jobs(order_p, 3, 2 * n_a + 3 * n_b + n_n),
                        **psum_jobs(order_q, 5, rounds_q, extra_q)}
            return {**psum_jobs(order_p, 3, 6 * t - 2), **psum_jobs(order_q, 5, 4 * t - 3, 1)}

        def bank_of(job, table):
            ring = (pp, p_full, p_empty) if job[0] in ("ht", "pt") else (pq, q_full, q_empty)
            n, use = table[job]
            return ring[0][n], ring[1][n], ring[2][n], use

        def run(engine, iteration):
            def flags(t):
                return 0 <= t < groups, 1 <= t <= groups, -1 <= t < groups, 2 <= t <= groups + 1
            for t in range(-1, 3):
                iteration(t, *flags(t))
            with engine.Fori(3, groups - 1) as t:
                iteration(t, True, True, True, True)
            for t in range(groups - 1, groups + 2):
                iteration(t, *flags(t))

        block = ctx.enter_context(nc.Block())

        @block.sync
        def _(sp):
            def load_x(src):
                sp.dma_start(xin[:], src).then_inc(x_loaded, 16)

            def load_adj(s, g):
                sp.dma_start(adj_tr[s][:], adj_t_g[g]).then_inc(adj_loaded[s], 16)
                sp.dma_start(adj_n[s][:], adj_g[g]).then_inc(adj_loaded[s], 16)

            def load_weights(s, w):
                src = (w_left, w_right, w_lin_t)[w][s].rearrange("(k p) n -> p k n", p=P)
                sp.dma_start(staging[3 * s + w], src).then_inc(w_loaded[3 * s + w], 16)

            def load_l1_weights(w):
                sp.dma_start(l1_staging[w], l1_weights[w].rearrange("(k p) n -> p k n", p=P)).then_inc(w_loaded[6 + w], 16)

            load_x(x_g[0])
            for w in range(3):
                load_weights(A, w)
            sp.dma_start(cols[:], ln_cols).then_inc(consts_loaded, 16)
            sp.dma_start(bias[:], b_lin.partition_broadcast(P)).then_inc(consts_loaded, 16)
            sp.dma_start(a1[:], ln_a1.partition_broadcast(P)).then_inc(consts_loaded, 16)
            sp.dma_start(b1[:], ln_b1.partition_broadcast(P)).then_inc(consts_loaded, 16)
            load_weights(B, 0)
            load_weights(B, 1)

            def iteration(t, a, b, n, f):
                at = isinstance(t, int)
                if n and not (at and t < 0):
                    sp.wait_ge(ht_lo_ready[A], KC * (t + 1))
                    load_x(x2_g[0] if at and t == groups - 1 else x_g[t + 1])
                if a:
                    if not at or t >= 1:
                        sp.wait_ge(e_ready[A], t)
                    load_adj(A, t)
                    if at and t == 0:
                        sp.wait_ge(w_ready, 3)
                        load_weights(B, 2)
                if b:
                    if not at or t >= 2:
                        sp.wait_ge(e_ready[B], t - 1)
                    load_adj(B, t - 1)
                if at and t == 2:
                    for buf, src in zip(kept["l1_consts"], l1_consts):
                        sp.dma_start(buf[:], src.partition_broadcast(P)).then_inc(l1_consts_loaded, 16)
                if at and t == groups:
                    sp.wait_ge(ht_lo_ready[A], KC * (groups + 1))
                    load_l1_weights(0)
                    sp.wait_ge(ht_lo_ready[B], KC * groups)
                    load_l1_weights(1)
                    sp.wait_ge(w_ready, 7)
                    load_l1_weights(2)
                if f and not (at and t == groups + 1):
                    sp.wait_ge(x2_ready, t - 1)
                    sp.dma_start(x2_g[t - 2], xres[:]).then_inc(x2_stored, 16)
                    sp.wait_ge(x2_stored, 16 * (t - 1))
                if b:
                    if at and t == 1:
                        sp.wait_ge(w_ready, 6)
                    sp.dma_start(xres[:], x_g[t - 1]).then_inc(xres_loaded, 16)

            run(sp, iteration)
            sp.wait_ge(l1_consts_loaded, 16 * len(l1_consts))
            sp.wait_ge(xres_loaded, 16 * groups)

        @block.tensor
        def _(pe):
            def open_bank(job, table):
                bank, full, empty, use = bank_of(job, table)
                if not isinstance(use, int) or use > 1:
                    pe.wait_ge(empty, use - 1)
                return bank, full

            def transposes(s, table, src):
                for k in range(KC):
                    bank, full = open_bank(("ht", s, k), table)
                    for i in range(G):
                        mm = pe.transpose(bank[:, i * S:(i + 1) * S], src[:, i, k * P:(k + 1) * P], ident[:])
                    mm.then_inc(full, 1)

            def split_product(out, pairs):
                last = len(pairs) - 1
                for n, ((l_hi, l_lo), (r_hi, r_lo)) in enumerate(pairs):
                    pe.matmul(out, l_hi, r_hi, start=(n == 0), stop=False)
                    pe.matmul(out, l_hi, r_lo, start=False, stop=False)
                    mm = pe.matmul(out, l_lo, r_hi, start=False, stop=(n == last))
                return mm

            def project(s, table):
                for j in range(2 * KC):
                    m, w = j // 2, j % 2
                    bank, full = open_bank(("pt", s, j), table)
                    cut = slice(m * P, (m + 1) * P)
                    split_product(bank[:], [
                        ((w_hi[s][w][:, k, cut], w_lo[s][w][:, k, cut]), (ht_hi[s][:, k, :], ht_lo[s][:, k, :]))
                        for k in range(KC)]).then_inc(full, 1)

            def values(s, graphs, table):
                for i in graphs:
                    bank, full = open_bank(("val", s, i), table)
                    cut = slice(i * S, (i + 1) * S)
                    split_product(bank[:, 0:H], [
                        ((ht_hi[s][:, k, cut], ht_lo[s][:, k, cut]), (w_hi[s][2][:, k, :], w_lo[s][2][:, k, :]))
                        for k in range(KC)]).then_inc(full, 1)

            def scores(s, table):
                for half in range(2):
                    bank, full = open_bank(("u", s, half), table)
                    for i in (2 * half, 2 * half + 1):
                        cut = slice(i * S, (i + 1) * S)
                        at = (i % 2) * 2 * S
                        mm = split_product(bank[:, at:at + 2 * S].rearrange("p (w i) -> p w i", w=2), [
                            ((ht_hi[s][:, k, cut], ht_lo[s][:, k, cut]), (pt_hi[:, k, :, cut], pt_lo[:, k, :, cut]))
                            for k in range(KC)])
                    mm.then_inc(full, 1)

            def context(s, g, table):
                pe.wait_ge(e_lo_ready[s], g + 1)
                for i in range(G):
                    pe.wait_ge(val_lo_ready[s], G * g + i + 1)
                    bank, full = open_bank(("ctx", s, i), table)
                    split_product(bank[:, 0:HV], [
                        ((eu_hi[:, i, :], eu_lo[:, i, :]), (val_hi[:, i, :], val_lo[:, i, :]))]).then_inc(full, 1)

            pe.wait_ge(ident_ready, 1)

            def iteration(t, a, b, n, f):
                table = jobs(t, a, b, n, f)
                if isinstance(t, int) and t == 0:
                    pe.wait_ge(w_ready, 2)
                if isinstance(t, int) and t == 1:
                    pe.wait_ge(w_ready, 6)
                if a:
                    pe.wait_ge(ht_lo_ready[A], KC * (t + 1))
                    project(A, table)
                if f:
                    context(B, t - 2, table)
                if b:
                    pe.wait_ge(z_ready[B], t)
                    transposes(B, table, c[A])
                if a:
                    if isinstance(t, int) and t == 0:
                        pe.wait_ge(w_ready, 3)
                    values(A, (0, 1), table)
                    _, _, empty, use = bank_of(("pt", A, 2 * KC - 1), table)
                    pe.wait_ge(empty, use)
                    scores(A, table)
                    values(A, (2, 3), table)
                if b:
                    pe.wait_ge(ht_lo_ready[B], KC * t)
                    project(B, table)
                if a:
                    context(A, t, table)
                if b:
                    _, _, empty, use = bank_of(("pt", B, 2 * KC - 1), table)
                    pe.wait_ge(empty, use)
                    scores(B, table)
                    values(B, (0,), table)
                if n:
                    pe.wait_ge(z_ready[A], t + 2)
                    transposes(A, table, xin)
                if b:
                    values(B, (1, 2, 3), table)

            run(pe, iteration)

        @block.scalar
        def _(act):
            def turned(s, table):
                for k in range(KC):
                    bank, full, empty, use = bank_of(("ht", s, k), table)
                    act.wait_ge(full, use)
                    affine = {} if s == A else {"scale": cols[:, 0, k:k + 1], "bias": cols[:, 1, k:k + 1]}
                    act.activation(ht_hi[s][:, k, :], bank[:], ACT.Relu, **affine)
                    act.activation(ht[s][:, k, :], bank[:], ACT.Relu, **affine).then_inc(empty, 1)

            def pt_high(s, js, table):
                for j in js:
                    bank, full, _, use = bank_of(("pt", s, j), table)
                    act.wait_ge(full, use)
                    act.copy(pt_hi[:, j // 2, j % 2, :], bank[:]).then_inc(pt_hi_ready[s], 1)

            def val_high(s, graphs, table):
                for i in graphs:
                    _, _, empty, use = bank_of(("val", s, i), table)
                    act.wait_ge(empty, use)
                    act.copy(val_hi[:, i, 0:H], val[:, i, :]).then_inc(val_hi_ready[s], 1)

            def exponential(s, g):
                act.wait_ge(scores_summed[s], g + 1)
                act.activation(eu[:], eu[:], ACT.Exp, scale=1.0 / TEMPER).then_inc(exp_ready[s], 1)

            def e_high(s, g):
                act.wait_ge(e_ready[s], g + 1)
                act.copy(eu_hi[:], eu[:]).then_inc(e_hi_ready[s], 1)

            def context_out(s, table):
                for i in range(G):
                    bank, full, empty, use = bank_of(("ctx", s, i), table)
                    act.wait_ge(full, use)
                    act.copy(c[s][:, i, :], bank[:, 0:HV]).then_inc(empty, 1)

            def context_scale(s, g, table):
                _, _, empty, use = bank_of(("ctx", s, G - 1), table)
                act.wait_ge(empty, use)
                act.wait_ge(rsum_ready[s], g + 1)
                for i in range(G):
                    act.activation(c[s][:, i, 0:H], c[s][:, i, 0:H], ACT.Copy,
                                   scale=rsum[s][:, 1, i:i + 1]).then_inc(c_scaled[s], 1)

            act.wait_ge(consts_loaded, 4 * 16)

            def iteration(t, a, b, n, f):
                table = jobs(t, a, b, n, f)
                if a:
                    pt_high(A, range(2 * KC), table)
                if f:
                    if not isinstance(t, int) or t >= 3:
                        act.wait_ge(x2_ready, t - 2)
                    context_out(B, table)
                if b:
                    turned(B, table)
                if f:
                    context_scale(B, t - 2, table)
                if a:
                    val_high(A, range(G), table)
                    exponential(A, t)
                if b:
                    pt_high(B, range(0, 2), table)
                if a:
                    e_high(A, t)
                if b:
                    pt_high(B, range(2, 2 * KC), table)
                if a:
                    context_out(A, table)
                    context_scale(A, t, table)
                if b:
                    val_high(B, (0,), table)
                if n:
                    turned(A, table)
                if b:
                    exponential(B, t - 1)
                    val_high(B, (1,), table)
                    e_high(B, t - 1)
                    val_high(B, (2, 3), table)

            run(act, iteration)

        @block.vector
        def _(dve):
            def moments(s, g, src, step):
                for i in range(G):
                    if step is not None:
                        dve.wait_ge(step, G * g + i + 1)
                    bn = dve.bn_stats(stats[s][:, i, :], src[:, i, 0:H])
                bn.then_inc(bn_ready[s], 1)
                dve.wait_ge(consts_set, 1)
                dve.wait_ge(bn_ready[s], g + 1)
                for i in range(G):
                    ag = dve.bn_aggr(mv[s][:, i, :], stats[s][:, i, :])
                ag.then_inc(mv_ready[s], 1)

            def centre(s, g, src):
                dve.wait_ge(inv_ready[s], g + 1)
                for i in range(G):
                    z = dve.tensor_scalar(src[:, i, 0:H], src[:, i, 0:H], mv[s][:, i, 0:1],
                                          inv[s][:, 3, i:i + 1], ALU.subtract, ALU.mult)
                return z

            def turned_low(s, table):
                for k in range(KC):
                    _, _, empty, use = bank_of(("ht", s, k), table)
                    dve.wait_ge(empty, use)
                    dve.tensor_tensor(ht_lo[s][:, k, :], ht[s][:, k, :], ht_hi[s][:, k, :].bitcast(F32),
                                      ALU.subtract).then_inc(ht_lo_ready[s], 1)

            def pt_low(s, g, js, table):
                for j in js:
                    bank, _, empty, use = bank_of(("pt", s, j), table)
                    dve.wait_ge(pt_hi_ready[s], 2 * KC * g + j + 1)
                    dve.tensor_tensor(pt_lo[:, j // 2, j % 2, :], bank[:], pt_hi[:, j // 2, j % 2, :].bitcast(F32),
                                      ALU.subtract).then_inc(empty, 1)

            def values_out(s, graphs, table, free, free_count):
                for i in graphs:
                    bank, full, empty, use = bank_of(("val", s, i), table)
                    dve.wait_ge(full, use)
                    if free is not None:
                        dve.wait_ge(free, free_count + i)
                    dve.tensor_tensor(val[:, i, :], bank[:, 0:H], bias[:, s, :], ALU.add).then_inc(empty, 1)

            def masked(s, g, table):
                dve.wait_ge(masks_ready[s], g + 1)
                for half in range(2):
                    bank, full, empty, use = bank_of(("u", s, half), table)
                    dve.wait_ge(full, use)
                    two = slice(2 * half, 2 * half + 2)
                    u = bank[:].rearrange("p (b w i) -> p b w i", b=2, w=2)
                    dve.tensor_tensor(um[:, 0, two, :], u[:, :, 0, :], m_left[s][:, two, :], ALU.mult)
                    dve.tensor_tensor(um[:, 1, two, :], u[:, :, 1, :], m_right[s][:, two, :], ALU.mult).then_inc(empty, 1)

            def e_low(s, g):
                dve.wait_ge(e_hi_ready[s], g + 1)
                dve.tensor_tensor(eu_lo[:], eu[:], eu_hi[:].bitcast(F32), ALU.subtract).then_inc(e_lo_ready[s], 1)

            def inverse_sums(s, g, table):
                _, _, empty, use = bank_of(("ctx", s, G - 1), table)
                dve.wait_ge(empty, use)
                dve.tensor_scalar(rsum[s][:, 0, :], c[s][:, :, H], SUM_EPS, None, ALU.add).then_inc(rsum_eps[s], 1)
                dve.wait_ge(rsum_eps[s], g + 1)
                dve.reciprocal(rsum[s][:, 1, :], rsum[s][:, 0, :]).then_inc(rsum_ready[s], 1)

            for n, number in enumerate(NUMBERS):
                dve.memset(num[:, n, :], number)
            dve.memset(val_hi[:, :, H:H + 1].bitcast(F32), 1.0)
            dve.memset(val_hi[:, :, H + 1:HV].bitcast(F32), 0.0)
            dve.memset(val_lo[:, :, H:HV].bitcast(F32), 0.0).then_inc(consts_set, 1)

            def front(g):
                dve.wait_ge(x_loaded, 16 * (g + 1))
                moments(2, g, xin, None)

            def split_weights(n, w_hi, w_lo, staged):
                dve.wait_ge(w_loaded[n], 16)
                dve.tensor_copy(w_hi[:], staged).then_inc(w_hi_ready, 1)
                dve.wait_ge(w_hi_ready, n + 1)
                dve.tensor_tensor(w_lo[:], staged, w_hi[:].bitcast(F32), ALU.subtract).then_inc(w_ready, 1)

            def split_l1_weights(w):
                split_weights(6 + w, w_hi[A][w], w_lo[A][w], l1_staging[w])

            def iteration(t, a, b, n, f):
                table = jobs(t, a, b, n, f)
                at = isinstance(t, int)
                tail = at and t == groups + 1
                if at and t == 0:
                    for s in (A, B):
                        for w in range(3):
                            split_weights(3 * s + w, w_hi[s][w], w_lo[s][w], staging[3 * s + w])
                    dve.wait_ge(consts_loaded, 4 * 16)
                if a:
                    pt_low(A, t, range(0, 2), table)
                if b:
                    centre(A, t - 1, c[A]).then_inc(z_ready[B], 1)
                if a:
                    pt_low(A, t, range(2, 2 * KC), table)
                if f:
                    inverse_sums(B, t - 2, table)
                if b:
                    turned_low(B, table)
                if f and not tail:
                    moments(B, t - 2, c[B], c_scaled[B])
                if at and t == groups:
                    split_l1_weights(0)
                free = (val_lo_ready[B], G * (t - 2) + 1) if not at or t >= 2 else (None, 0)
                if a:
                    values_out(A, (0, 1), table, *free)
                    masked(A, t, table)
                    values_out(A, (2, 3), table, *free)
                if n:
                    front(t + 1)
                if b:
                    pt_low(B, t - 1, range(0, 2), table)
                if f and not tail:
                    centre(B, t - 2, c[B]).then_inc(fin_z, 1)
                if b:
                    pt_low(B, t - 1, range(2, 3), table)
                if a:
                    e_low(A, t)
                if at and t == groups:
                    split_l1_weights(1)
                if b:
                    pt_low(B, t - 1, range(3, 2 * KC), table)
                if at and t == groups:
                    split_l1_weights(2)
                if n:
                    centre(2, t + 1, xin).then_inc(z_ready[A], 1)
                if a:
                    inverse_sums(A, t, table)
                    moments(A, t, c[A], c_scaled[A])
                free = (val_lo_ready[A], G * t + 1) if not at or t < groups else (val_lo_ready[A], G * (groups - 1) + 1)
                if b:
                    masked(B, t - 1, table)
                    values_out(B, (0,), table, *free)
                if n:
                    turned_low(A, table)
                if b:
                    values_out(B, (1, 2, 3), table, *free)
                    e_low(B, t - 1)
                if f and not tail:
                    dve.wait_ge(fin_b, t - 1)
                    dve.wait_ge(xres_loaded, 16 * (t - 1))
                    dve.scalar_tensor_tensor(xres[:], c[B][:, :, 0:H], 0.0, xres[:], ALU.max,
                                             ALU.add).then_inc(x2_ready, 1)
            run(dve, iteration)

        @block.gpsimd
        def _(pool):
            pool.memset(ident[:], 0.0).then_inc(ident_zero, 1)
            pool.wait_ge(ident_zero, 1)
            pool.affine_select(out=ident[:], in_=ident[:], compare_op=ALU.not_equal, fill=1.0, base=0,
                               pattern=[[-1, P]], channel_multiplier=1).then_inc(ident_ready, 1)
            pool.memset(after[:], 1.0).then_inc(ident_zero, 1)
            pool.wait_ge(ident_zero, 2)
            pool.affine_select(out=after[:], in_=after[:], compare_op=ALU.is_gt, fill=0.0, base=0,
                               pattern=[[1, P]], channel_multiplier=-1).then_inc(ident_ready, 1)
            pool.wait_ge(ident_ready, 2)
            pool.wait_ge(consts_set, 1)

            def masks(s, g):
                pool.wait_ge(adj_loaded[s], 32 * (g + 1))
                pool.tensor_tensor(m_right[s][:], adj_n[s][:], after[:, None, :].to_broadcast([P, G, S]), ALU.mult)
                pool.affine_select(out=m_left[s][:], in_=adj_tr[s][:], compare_op=ALU.is_ge, fill=0.0, base=0,
                                   pattern=[[0, G], [-1, S]], channel_multiplier=1).then_inc(masks_ready[s], 1)

            def front_inverse(g):
                pool.wait_ge(mv_ready[2], g + 1)
                pool.tensor_tensor(inv[2][:, 0, :], mv[2][:, :, 1], num[:, N_LN_EPS, :], ALU.add).then_inc(inv_step[2], 1)
                pool.wait_ge(inv_step[2], g + 1)
                pool.tensor_tensor(inv[2][:, 3, :], inv[2][:, 0, :], num[:, RSQRT, :], ALU.pow).then_inc(inv_ready[2], 1)

            def sigma_inverse(s, g):
                pool.wait_ge(mv_ready[s], g + 1)
                pool.tensor_tensor(inv[s][:, 0, :], mv[s][:, :, 1], num[:, N_UNBIAS, :], ALU.mult).then_inc(inv_step[s], 1)
                pool.wait_ge(inv_step[s], 3 * g + 1)
                pool.tensor_tensor(inv[s][:, 1, :], inv[s][:, 0, :], num[:, SQRT, :], ALU.pow).then_inc(inv_step[s], 1)
                pool.wait_ge(inv_step[s], 3 * g + 2)
                pool.tensor_tensor(inv[s][:, 2, :], inv[s][:, 1, :], num[:, N_L0_EPS, :], ALU.add).then_inc(inv_step[s], 1)
                pool.wait_ge(inv_step[s], 3 * g + 3)
                pool.tensor_tensor(inv[s][:, 3, :], inv[s][:, 2, :], num[:, RECIP, :], ALU.pow).then_inc(inv_ready[s], 1)

            def values_low(s, g, graphs):
                for i in graphs:
                    pool.wait_ge(val_hi_ready[s], G * g + i + 1)
                    pool.tensor_tensor(val_lo[:, i, 0:H], val[:, i, :], val_hi[:, i, 0:H].bitcast(F32),
                                       ALU.subtract).then_inc(val_lo_ready[s], 1)

            def sum_scores(s, g, table):
                _, _, empty, use = bank_of(("u", s, 1), table)
                pool.wait_ge(empty, use)
                pool.tensor_tensor(eu[:], um[:, 0], um[:, 1], ALU.add).then_inc(scores_summed[s], 1)

            def mask_exp(s, g):
                pool.wait_ge(exp_ready[s], g + 1)
                pool.tensor_tensor(eu[:], eu[:], adj_tr[s][:], ALU.mult).then_inc(e_ready[s], 1)

            def end_affine(g):
                pool.wait_ge(fin_z, g + 1)
                pool.tensor_tensor(c[B][:, :, 0:H], c[B][:, :, 0:H], a1[:, None, :].to_broadcast([P, G, H]),
                                   ALU.mult).then_inc(fin_a, 1)
                pool.wait_ge(fin_a, g + 1)
                pool.tensor_tensor(c[B][:, :, 0:H], c[B][:, :, 0:H], b1[:, None, :].to_broadcast([P, G, H]),
                                   ALU.add).then_inc(fin_b, 1)

            def iteration(t, a, b, n, f):
                table = jobs(t, a, b, n, f)
                tail = isinstance(t, int) and t == groups + 1
                if a:
                    masks(A, t)
                if b:
                    masks(B, t - 1)
                if a:
                    values_low(A, t, (0, 1))
                    sum_scores(A, t, table)
                if f and not tail:
                    sigma_inverse(B, t - 2)
                if a:
                    values_low(A, t, (2, 3))
                    mask_exp(A, t)
                if n:
                    front_inverse(t + 1)
                if f and not tail:
                    end_affine(t - 2)
                if b:
                    sum_scores(B, t - 1, table)
                    values_low(B, t - 1, (0,))
                    mask_exp(B, t - 1)
                    values_low(B, t - 1, (1, 2, 3))
                if a:
                    sigma_inverse(A, t)

            run(pool, iteration)


def l1_phase(nc, kept, x2, adj_t, out):
    n_graphs, S, H = x2.shape
    groups = n_graphs // G
    KC = H // P
    GS = G * S
    HV = H + 2
    SUM_EPS = 1e-10
    SCALE = 1.0 / float(H) ** 0.5
    FRONT, END, TAIL = 0, 1, 2
    LEFT, RIGHT, SELF = 0, 1, 2

    with ExitStack() as ctx:
        def sb(name, shape, dt=F32):
            return ctx.enter_context(nc.sbuf_tensor("l1_" + name, shape, dt))

        def sem(name):
            return ctx.enter_context(nc.semaphore("l1_" + name))

        def sems(name, n=2):
            return [sem(f"{name}{i}") for i in range(n)]

        w_hi, w_lo, ident, xin = kept["w_hi"], kept["w_lo"], kept["ident"], kept["xin"]
        ht, ht_hi, ht_lo = kept["ht"], kept["ht_hi"], kept["ht_lo"]
        bias, gam, bet = kept["l1_consts"]
        num = kept["num"]
        tail_x, tail_c, a1, b1 = kept["xres"], kept["c"], kept["a1"], kept["b1"]
        xres = sb("xres", [P, G, H])
        adj_tr = sb("adj_tr", [P, G, S])
        m_lr = sb("m_lr", [P, 2, G, S])
        m_self = sb("m_self", [P, G, S])
        val = [sb(f"val{w}", [P, G, H]) for w in (LEFT, RIGHT)]
        val_hi = [sb(f"val_hi{w}", [P, G, HV], F32R) for w in (LEFT, RIGHT)]
        val_lo = [sb(f"val_lo{w}", [P, G, HV], F32R) for w in (LEFT, RIGHT)]
        own = sb("own", [P, G, HV])
        neg_max = sb("neg_max", [P, 2, G])
        e = sb("e", [P, G, S])
        e_diag = sb("e_diag", [P, G, S])
        z_sum = sb("z_sum", [P, G])
        diag = sb("diag", [P, G])
        et = sb("et", [P, 2, G, S])
        et_hi = sb("et_hi", [P, 2, G, S], F32R)
        et_lo = sb("et_lo", [P, 2, G, S], F32R)
        c = sb("c", [P, G, HV])
        zc = sb("zc", [P, G, H])
        q = sb("q", [P, 4, G])
        stats = [sb(f"stats{n}", [P, G, 6]) for n in (FRONT, END, TAIL)]
        mv = [sb(f"mv{n}", [P, G, 2]) for n in (FRONT, END, TAIL)]
        inv = [sb(f"inv{n}", [P, 4, G]) for n in (FRONT, END, TAIL)]

        ps = [ctx.enter_context(nc.psum_tensor("l1_ps", [P, 512], F32))]
        pp = [ctx.enter_context(nc.psum_tensor(f"l1_pp{i}", [P, 512], F32)) for i in range(KC)]
        pq = [ctx.enter_context(nc.psum_tensor(f"l1_pq{i}", [P, 512], F32)) for i in range(G)]
        s_full, s_empty = sems("s_full", 1), sems("s_empty", 1)
        p_full, p_empty = sems("p_full", KC), sems("p_empty", KC)
        q_full, q_empty = sems("q_full", G), sems("q_empty", G)

        consts_set = sem("consts_set")
        x_loaded, xres_loaded, adj_loaded = sem("x_loaded"), sem("xres_loaded"), sem("adj_loaded")
        masks_ready = sem("masks_ready")
        bn_ready, mv_ready = sems("bn_ready", 3), sems("mv_ready", 3)
        inv_step, inv_ready = sems("inv_step", 3), sems("inv_ready", 3)
        z_ready, ht_ready = sems("z_ready"), sem("ht_ready")
        max_ready, bias_ready = sem("max_ready"), sem("bias_ready")
        diag_masked, diag_ready = sem("diag_masked"), sem("diag_ready")
        et_hi_ready, et_lo_ready = sem("et_hi_ready"), sem("et_lo_ready")
        val_hi_ready, val_lo_ready = sem("val_hi_ready"), sem("val_lo_ready")
        q_ready = sem("q_ready")
        tail_centred, tail_scaled, tail_shifted = sem("tail_centred"), sem("tail_scaled"), sem("tail_shifted")
        tail_ready, tail_stored = sem("tail_ready"), sem("tail_stored")
        scaled, shifted, out_ready, out_stored = sem("scaled"), sem("shifted"), sem("out_ready"), sem("out_stored")

        x_g = x2.rearrange("(g b) s h -> g s b h", b=G)
        out_g = out.rearrange("(g b) s h -> g s b h", b=G)
        adj_t_g = adj_t.rearrange("(g b) j i -> g j b i", b=G)

        def jobs(t, a, n):
            table = {}
            if n:
                table |= psum_jobs([("ht", k) for k in range(KC)], KC, t)
            if a:
                table |= psum_jobs([("u", 0), ("et", 0)], 1, 2 * t)
                table |= psum_jobs([("val", w, i) for w in (LEFT, RIGHT, SELF) for i in range(G)] +
                                   [("ctx", i) for i in range(G)], G, 4 * t)
            return table

        def bank_of(job, table):
            if job[0] in ("u", "et"):
                ring = (ps, s_full, s_empty)
            elif job[0] == "ht":
                ring = (pp, p_full, p_empty)
            else:
                ring = (pq, q_full, q_empty)
            n, use = table[job]
            return ring[0][n], ring[1][n], ring[2][n], use

        def run(engine, iteration):
            iteration(0, True, True, False, False)
            iteration(1, True, True, True, False)
            iteration(2, True, True, True, True)
            with engine.Fori(3, groups - 1) as t:
                iteration(t, True, True, True, True)
            iteration(groups - 1, True, False, True, True)
            iteration(groups, False, False, True, True)
            iteration(groups + 1, False, False, False, True)

        block = ctx.enter_context(nc.Block())

        @block.sync
        def _(sp):
            def iteration(t, a, n, f, o):
                if n:
                    if not isinstance(t, int) or t >= 1:
                        sp.wait_ge(ht_ready, KC * t)
                    sp.dma_start(xin[:], x_g[t + 1]).then_inc(x_loaded, 16)
                if a:
                    if not isinstance(t, int) or t >= 1:
                        sp.wait_ge(masks_ready, t)
                    sp.dma_start(adj_tr[:], adj_t_g[t]).then_inc(adj_loaded, 16)
                if isinstance(t, int) and t == 1:
                    sp.wait_ge(tail_ready, 1)
                    sp.dma_start(x_g[groups - 1], tail_x[:]).then_inc(tail_stored, 16)
                    sp.wait_ge(tail_stored, 16)
                if o:
                    sp.wait_ge(out_ready, t - 1)
                    sp.dma_start(out_g[t - 2], xres[:]).then_inc(out_stored, 16)
                    sp.wait_ge(out_stored, 16 * (t - 1))
                if f:
                    sp.dma_start(xres[:], x_g[t - 1]).then_inc(xres_loaded, 16)

            run(sp, iteration)

        @block.tensor
        def _(pe):
            def open_bank(job, table):
                bank, full, empty, use = bank_of(job, table)
                if not isinstance(use, int) or use > 1:
                    pe.wait_ge(empty, use - 1)
                return bank, full

            def split_product(out_ap, pairs):
                last = len(pairs) - 1
                for n, ((l_hi, l_lo), (r_hi, r_lo)) in enumerate(pairs):
                    pe.matmul(out_ap, l_hi, r_hi, start=(n == 0), stop=False)
                    pe.matmul(out_ap, l_hi, r_lo, start=False, stop=False)
                    mm = pe.matmul(out_ap, l_lo, r_hi, start=False, stop=(n == last))
                return mm

            def scores(table):
                bank, full = open_bank(("u", 0), table)
                for i in range(G):
                    cut = slice(i * S, (i + 1) * S)
                    for k in range(KC):
                        mm = pe.matmul(bank[:, cut], ht[:, k, cut], ht[:, k, cut], start=(k == 0), stop=(k == KC - 1))
                mm.then_inc(full, 1)

            def values(w, table):
                for i in range(G):
                    bank, full = open_bank(("val", w, i), table)
                    cut = slice(i * S, (i + 1) * S)
                    split_product(bank[:, 0:H], [
                        ((ht_hi[:, k, cut], ht_lo[:, k, cut]), (w_hi[w][:, k, :], w_lo[w][:, k, :]))
                        for k in range(KC)]).then_inc(full, 1)

            def iteration(t, a, n, f, o):
                table = jobs(t, a, n)
                if a:
                    if not isinstance(t, int) or t >= 1:
                        pe.wait_ge(ht_ready, KC * t)
                    scores(table)
                    values(LEFT, table)
                    bank, full = open_bank(("et", 0), table)
                    for i in range(G):
                        mm = pe.transpose(bank[:, i * S:(i + 1) * S], e[:, i, :], ident[:])
                    mm.then_inc(full, 1)
                    values(RIGHT, table)
                    values(SELF, table)
                if n:
                    pe.wait_ge(z_ready[FRONT], t + 1)
                    for k in range(KC):
                        bank, full = open_bank(("ht", k), table)
                        for i in range(G):
                            mm = pe.transpose(bank[:, i * S:(i + 1) * S], xin[:, i, k * P:(k + 1) * P], ident[:])
                        mm.then_inc(full, 1)
                if a:
                    pe.wait_ge(et_lo_ready, t + 1)
                    pe.wait_ge(val_lo_ready, 2 * G * (t + 1))
                    for i in range(G):
                        bank, full = open_bank(("ctx", i), table)
                        split_product(bank[:, 0:HV], [
                            ((et_hi[:, w, i, :], et_lo[:, w, i, :]), (val_hi[w][:, i, :], val_lo[w][:, i, :]))
                            for w in (LEFT, RIGHT)]).then_inc(full, 1)

            run(pe, iteration)

        @block.scalar
        def _(act):
            def values_high(w, t, table):
                for i in range(G):
                    _, _, empty, use = bank_of(("val", w, i), table)
                    act.wait_ge(empty, use)
                    act.copy(val_hi[w][:, i, 0:H], val[w][:, i, :]).then_inc(val_hi_ready, 1)

            def centre(n, g, buf, z_buf):
                act.wait_ge(inv_ready[n], g + 1)
                for i in range(G):
                    z = act.activation(z_buf[:, i, 0:H], buf[:, i, 0:H], ACT.Identity, scale=inv[n][:, 3, i:i + 1],
                                       bias=inv[n][:, 2, i:i + 1])
                z.then_inc(z_ready[n], 1)

            def iteration(t, a, n, f, o):
                table = jobs(t, a, n)
                if a:
                    bank, full, empty, use = bank_of(("u", 0), table)
                    act.wait_ge(bias_ready, t + 1)
                    for i in range(G):
                        ex = act.activation(e[:, i, :], bank[:, i * S:(i + 1) * S], ACT.Exp, scale=SCALE,
                                            bias=neg_max[:, 1, i:i + 1], accum_out=z_sum[:, i:i + 1])
                    ex.then_inc(empty, 1)
                    values_high(LEFT, t, table)
                if f:
                    if not isinstance(t, int) or t >= 2:
                        act.wait_ge(out_ready, t - 1)
                    centre(END, t - 1, c, zc)
                if a:
                    _, _, empty, use = bank_of(("et", 0), table)
                    act.wait_ge(empty, use)
                    act.copy(et_hi[:], et[:]).then_inc(et_hi_ready, 1)
                    values_high(RIGHT, t, table)
                if n:
                    centre(FRONT, t, xin, xin)
                    for k in range(KC):
                        bank, full, empty, use = bank_of(("ht", k), table)
                        act.wait_ge(full, use)
                        act.activation(ht_hi[:, k, :], bank[:], ACT.Relu)
                        act.activation(ht[:, k, :], bank[:], ACT.Relu).then_inc(empty, 1)

            run(act, iteration)

        @block.vector
        def _(dve):
            def moments(n, g, src):
                for i in range(G):
                    bn = dve.bn_stats(stats[n][:, i, :], src[:, i, 0:H])
                bn.then_inc(bn_ready[n], 1)
                dve.wait_ge(consts_set, 1)
                dve.wait_ge(bn_ready[n], g + 1)
                for i in range(G):
                    ag = dve.bn_aggr(mv[n][:, i, :], stats[n][:, i, :])
                ag.then_inc(mv_ready[n], 1)

            def values_out(w, t, table):
                for i in range(G):
                    bank, full, empty, use = bank_of(("val", w, i), table)
                    dve.wait_ge(full, use)
                    if w == SELF:
                        dve.tensor_tensor(own[:, i, 0:H], bank[:, 0:H], bias[:, w, :], ALU.add).then_inc(empty, 1)
                    else:
                        dve.tensor_tensor(val[w][:, i, :], bank[:, 0:H], bias[:, w, :], ALU.add).then_inc(empty, 1)

            dve.memset(own[:, :, H:HV], 1.0)
            for w in (LEFT, RIGHT):
                dve.memset(val_hi[w][:, :, H:H + 1].bitcast(F32), 1.0)
                dve.memset(val_hi[w][:, :, H + 1:HV].bitcast(F32), 0.0)
                last = dve.memset(val_lo[w][:, :, H:HV].bitcast(F32), 0.0)
            last.then_inc(consts_set, 1)

            def iteration(t, a, n, f, o):
                table = jobs(t, a, n)
                if a:
                    bank, full, _, use = bank_of(("u", 0), table)
                    dve.wait_ge(full, use)
                    dve.tensor_reduce(neg_max[:, 0, :], bank[:].rearrange("p (b j) -> p b j", b=G), AX_X, ALU.max,
                                      negate=True).then_inc(max_ready, 1)
                    dve.wait_ge(max_ready, t + 1)
                    dve.tensor_scalar(neg_max[:, 1, :], neg_max[:, 0, :], SCALE, None, ALU.mult).then_inc(bias_ready, 1)
                if o:
                    dve.wait_ge(shifted, t - 1)
                    dve.wait_ge(xres_loaded, 16 * (t - 1))
                    dve.scalar_tensor_tensor(xres[:], zc[:], 0.0, xres[:], ALU.max, ALU.add).then_inc(out_ready, 1)
                if f:
                    moments(END, t - 1, c)
                if isinstance(t, int) and t == 0:
                    moments(TAIL, 0, tail_c)
                if isinstance(t, int) and t == 1:
                    dve.wait_ge(tail_shifted, 1)
                    dve.scalar_tensor_tensor(tail_x[:], tail_c[:, :, 0:H], 0.0, tail_x[:], ALU.max,
                                             ALU.add).then_inc(tail_ready, 1)
                if a:
                    values_out(LEFT, t, table)
                if n:
                    dve.wait_ge(x_loaded, 16 * (t + 1))
                    moments(FRONT, t, xin)
                if isinstance(t, int) and t == 0:
                    dve.wait_ge(inv_ready[TAIL], 1)
                    for i in range(G):
                        z = dve.tensor_scalar(tail_c[:, i, 0:H], tail_c[:, i, 0:H], mv[TAIL][:, i, 0:1],
                                              inv[TAIL][:, 3, i:i + 1], ALU.subtract, ALU.mult)
                    z.then_inc(tail_centred, 1)
                if a:
                    bank, full, empty, use = bank_of(("et", 0), table)
                    dve.wait_ge(full, use)
                    dve.wait_ge(masks_ready, t + 1)
                    turned = bank[:].rearrange("p (b i) -> p b i", b=G)
                    dve.tensor_tensor(et[:, LEFT], turned, m_lr[:, LEFT], ALU.mult)
                    dve.tensor_tensor(et[:, RIGHT], turned, m_lr[:, RIGHT], ALU.mult).then_inc(empty, 1)
                    dve.wait_ge(diag_masked, t + 1)
                    dve.tensor_reduce(diag[:], e_diag[:], AX_X, ALU.add).then_inc(diag_ready, 1)
                    values_out(RIGHT, t, table)
                    dve.wait_ge(et_hi_ready, t + 1)
                    dve.tensor_tensor(et_lo[:], et[:], et_hi[:].bitcast(F32), ALU.subtract).then_inc(et_lo_ready, 1)
                if a:
                    values_out(SELF, t, table)
                if n:
                    for k in range(KC):
                        _, _, empty, use = bank_of(("ht", k), table)
                        dve.wait_ge(empty, use)
                        dve.tensor_tensor(ht_lo[:, k, :], ht[:, k, :], ht_hi[:, k, :].bitcast(F32),
                                          ALU.subtract).then_inc(ht_ready, 1)
                if a:
                    if not isinstance(t, int) or t >= 1:
                        dve.wait_ge(z_ready[END], t)
                    dve.wait_ge(diag_ready, t + 1)
                    _, _, own_landed, own_use = bank_of(("val", SELF, G - 1), table)
                    dve.wait_ge(own_landed, own_use)
                    for i in range(G):
                        bank, full, empty, use = bank_of(("ctx", i), table)
                        dve.wait_ge(full, use)
                        dve.scalar_tensor_tensor(c[:, i, 0:H + 1], own[:, i, 0:H + 1], diag[:, i:i + 1],
                                                 bank[:, 0:H + 1], ALU.mult, ALU.add).then_inc(empty, 1)
                    dve.wait_ge(empty, use)
                    dve.scalar_tensor_tensor(q[:, 0, :], z_sum[:], SUM_EPS, c[:, :, H], ALU.mult,
                                             ALU.add).then_inc(q_ready, 1)

            run(dve, iteration)

        @block.gpsimd
        def _(pool):
            pool.wait_ge(consts_set, 1)

            def inverse(n, step0):
                pool.tensor_tensor(inv[n][:, 3, :], inv[n][:, 0, :], num[:, RSQRT, :], ALU.pow).then_inc(inv_step[n], 1)
                pool.wait_ge(inv_step[n], step0 + 1)
                pool.tensor_tensor(inv[n][:, 1, :], inv[n][:, 3, :], mv[n][:, :, 0], ALU.mult).then_inc(inv_step[n], 1)
                pool.wait_ge(inv_step[n], step0 + 2)
                pool.tensor_tensor(inv[n][:, 2, :], inv[n][:, 1, :], num[:, RECIP, :], ALU.mult).then_inc(inv_ready[n], 1)

            def front_inverse(g):
                pool.wait_ge(mv_ready[FRONT], g + 1)
                pool.tensor_tensor(inv[FRONT][:, 0, :], mv[FRONT][:, :, 1], num[:, N_LN_EPS, :],
                                   ALU.add).then_inc(inv_step[FRONT], 1)
                pool.wait_ge(inv_step[FRONT], 3 * g + 1)
                inverse(FRONT, 3 * g + 1)

            def end_inverse(g):
                pool.wait_ge(mv_ready[END], g + 1)
                pool.wait_ge(q_ready, g + 1)
                pool.tensor_tensor(q[:, 1, :], q[:, 0, :], q[:, 0, :], ALU.mult).then_inc(inv_step[END], 1)
                pool.wait_ge(inv_step[END], 5 * g + 1)
                pool.tensor_tensor(q[:, 2, :], q[:, 1, :], num[:, N_L1_EPS, :], ALU.mult).then_inc(inv_step[END], 1)
                pool.wait_ge(inv_step[END], 5 * g + 2)
                pool.tensor_tensor(inv[END][:, 0, :], q[:, 2, :], mv[END][:, :, 1], ALU.add).then_inc(inv_step[END], 1)
                pool.wait_ge(inv_step[END], 5 * g + 3)
                inverse(END, 5 * g + 3)

            def tail_inverse():
                v, done = inv[TAIL], inv_step[TAIL]
                pool.wait_ge(mv_ready[TAIL], 1)
                pool.tensor_tensor(v[:, 0, :], mv[TAIL][:, :, 1], num[:, N_UNBIAS, :], ALU.mult).then_inc(done, 1)
                pool.wait_ge(done, 1)
                pool.tensor_tensor(v[:, 1, :], v[:, 0, :], num[:, SQRT, :], ALU.pow).then_inc(done, 1)
                pool.wait_ge(done, 2)
                pool.tensor_tensor(v[:, 2, :], v[:, 1, :], num[:, N_L0_EPS, :], ALU.add).then_inc(done, 1)
                pool.wait_ge(done, 3)
                pool.tensor_tensor(v[:, 3, :], v[:, 2, :], num[:, RECIP, :], ALU.pow).then_inc(inv_ready[TAIL], 1)

            def tail_affine():
                pool.wait_ge(tail_centred, 1)
                pool.tensor_tensor(tail_c[:, :, 0:H], tail_c[:, :, 0:H], a1[:, None, :].to_broadcast([P, G, H]),
                                   ALU.mult).then_inc(tail_scaled, 1)
                pool.wait_ge(tail_scaled, 1)
                pool.tensor_tensor(tail_c[:, :, 0:H], tail_c[:, :, 0:H], b1[:, None, :].to_broadcast([P, G, H]),
                                   ALU.add).then_inc(tail_shifted, 1)

            def values_low(w, t):
                for i in range(G):
                    pool.wait_ge(val_hi_ready, 2 * G * t + G * w + i + 1)
                    pool.tensor_tensor(val_lo[w][:, i, 0:H], val[w][:, i, :], val_hi[w][:, i, 0:H].bitcast(F32),
                                       ALU.subtract).then_inc(val_lo_ready, 1)

            def iteration(t, a, n, f, o):
                table = jobs(t, a, n)
                if a:
                    pool.wait_ge(adj_loaded, 16 * (t + 1))
                    pool.tensor_tensor(m_self[:], adj_tr[:], ident[:, None, :].to_broadcast([P, G, S]), ALU.mult)
                    for w, sign in ((LEFT, 1), (RIGHT, -1)):
                        sel = pool.affine_select(out=m_lr[:, w], in_=adj_tr[:], compare_op=ALU.is_gt, fill=0.0,
                                                 base=0, pattern=[[0, G], [-sign, S]], channel_multiplier=sign)
                    sel.then_inc(masks_ready, 1)
                if f:
                    end_inverse(t - 1)
                if isinstance(t, int) and t == 0:
                    tail_inverse()
                if a:
                    _, _, empty, use = bank_of(("u", 0), table)
                    pool.wait_ge(empty, use)
                    pool.wait_ge(masks_ready, t + 1)
                    pool.tensor_tensor(e_diag[:], e[:], m_self[:], ALU.mult).then_inc(diag_masked, 1)
                    values_low(LEFT, t)
                if n:
                    front_inverse(t)
                if a:
                    values_low(RIGHT, t)
                if isinstance(t, int) and t == 0:
                    tail_affine()
                if f:
                    pool.wait_ge(z_ready[END], t)
                    pool.tensor_tensor(zc[:], zc[:], gam[:, None, :].to_broadcast([P, G, H]),
                                       ALU.mult).then_inc(scaled, 1)
                    pool.wait_ge(scaled, t)
                    pool.tensor_tensor(zc[:], zc[:], bet[:, None, :].to_broadcast([P, G, H]),
                                       ALU.add).then_inc(shifted, 1)

            run(pool, iteration)


def build(nc, x, adj, adj_t, l0_w_left, l0_w_right, l0_w_lin_t, l0_b_lin, l0_ln_cols, l0_ln_a1, l0_ln_b1,
          l1_w_left_t, l1_w_self_t, l1_w_right_t, l1_biases, l1_gamma, l1_beta, out):
    H = x.shape[2]
    KC, GS = H // P, G * P
    x2 = nc.dram_tensor("x2_scratch", list(x.shape), F32, kind="Internal").ap()
    with ExitStack() as ctx:
        def sb(name, shape, dt=F32):
            return ctx.enter_context(nc.sbuf_tensor(name, shape, dt))

        kept = {
            "w_hi": [sb(f"kept_w_hi{w}", [P, KC, H], F32R) for w in range(3)],
            "w_lo": [sb(f"kept_w_lo{w}", [P, KC, H], F32R) for w in range(3)],
            "ident": sb("ident", [P, P]),
            "num": sb("num", [P, N_L1_EPS + 1, G]),
            "xin": sb("xin", [P, G, H]),
            "xres": sb("xres", [P, G, H]),
            "c": sb("c_b", [P, G, H + 2]),
            "a1": sb("a1", [P, H]),
            "b1": sb("b1", [P, H]),
            "ht": sb("ht", [P, KC, GS]),
            "ht_hi": sb("ht_hi", [P, KC, GS], F32R),
            "ht_lo": sb("ht_lo", [P, KC, GS], F32R),
            "l1_consts": [sb("l1_bias", [P, 3, H]), sb("l1_gamma", [P, H]), sb("l1_beta", [P, H])],
        }
        l0_phase(nc, kept, x, adj, adj_t, l0_w_left, l0_w_right, l0_w_lin_t, l0_b_lin, l0_ln_cols, l0_ln_a1,
                 l0_ln_b1, (l1_biases, l1_gamma, l1_beta), (l1_w_left_t, l1_w_right_t, l1_w_self_t), x2)
        l1_phase(nc, kept, x2, adj_t, out)


def kernel(**inputs):
    import numpy as np
    import concourse.bacc as bacc
    from concourse.bass_utils import run_bass_kernel_spmd

    i = {k: np.asarray(v) for k, v in inputs.items()}
    chunks = i["x"].shape[2] // P
    laid = {
        "x": i["x"],
        "adj": i["adj"],
        "adj_t": i["adj"].transpose(0, 2, 1),
        "l0_w_left": i["L0_gnn_W_left"],
        "l0_w_right": i["L0_gnn_W_right"],
        "l0_w_lin_t": i["L0_gnn_W_lin"].transpose(0, 2, 1),
        "l0_b_lin": i["L0_gnn_b_lin"],
        "l0_ln_cols": np.stack([i["L0_gnn_ln_a"][0].reshape(chunks, P).T, i["L0_gnn_ln_b"][0].reshape(chunks, P).T], 1),
        "l0_ln_a1": i["L0_gnn_ln_a"][1],
        "l0_ln_b1": i["L0_gnn_ln_b"][1],
        "l1_w_left_t": i["L1_gnn_W_left"].T,
        "l1_w_self_t": i["L1_gnn_W_self"].T,
        "l1_w_right_t": i["L1_gnn_W_right"].T,
        "l1_biases": np.stack([i["L1_gnn_b_left"], i["L1_gnn_b_right"], i["L1_gnn_b_self"]]),
        "l1_gamma": i["L1_gnn_gamma"],
        "l1_beta": i["L1_gnn_beta"],
    }
    nc = bacc.Bacc("TRN2", target_bir_lowering=False, num_devices=1)
    arrays, args = {}, []
    for name, a in laid.items():
        a = np.ascontiguousarray(a)
        arrays[f"in_{name}"] = a
        args.append(nc.dram_tensor(f"in_{name}", a.shape, mybir.dt.from_np(a.dtype), kind="ExternalInput").ap())
    args.append(nc.dram_tensor("out_0", i["x"].shape, mybir.dt.from_np(i["x"].dtype), kind="ExternalOutput").ap())
    build(nc, *args)
    r = run_bass_kernel_spmd(nc, [arrays], core_ids=[0])
    return r.results[0]["out_0"]
```

```python
from contextlib import ExitStack

import concourse.bass as bass
from concourse import mybir

F32 = mybir.dt.float32
F32R = mybir.dt.float32r
ALU = mybir.AluOpType
ACT = mybir.ActivationFunctionType
AX_X = mybir.AxisListType.X

P = 128
G = 4
A, B = 0, 1
FRONT = 2
LN_EPS = 1e-5
L0_EPS = 1e-3
L1_EPS = 1e-12
RSQRT, SQRT, MINUS_ONE, N_LN_EPS, N_UNBIAS, N_L0_EPS, N_L1_EPS = range(7)


def is_step(t, step):
    return isinstance(t, int) and t == step


def psum_jobs(order, banks, rounds, extra=0):
    return {job: ((extra + m) % banks, rounds + (extra + m) // banks + 1) for m, job in enumerate(order)}


def l0_phase(nc, kept, x, adj, adj_t, w_left, w_right, w_lin_t, b_lin, ln_cols, ln_a1, ln_b1, l1_consts,
             l1_weights, x2):
    n_graphs, S, H = x.shape
    groups = n_graphs // G
    KC = H // P
    GS = G * S
    HV = H + 2
    SUM_EPS = 1e-10
    TEMPER = float(H) ** 0.5
    NUMBERS = (-0.5, 0.5, -1.0, LN_EPS, H / (H - 1.0), L0_EPS, L1_EPS)
    assert S == P and H % P == 0

    with ExitStack() as ctx:
        def sb(name, shape, dt=F32):
            return ctx.enter_context(nc.sbuf_tensor(name, shape, dt))

        def sem(name):
            return ctx.enter_context(nc.semaphore("l0_" + name))

        def sems(name, n=2):
            return [sem(f"{name}{i}") for i in range(n)]

        w_hi = [kept["w_hi"], [sb(f"w_hi{w}", [P, KC, H], F32R) for w in range(3)]]
        w_lo = [kept["w_lo"], [sb(f"w_lo{w}", [P, KC, H], F32R) for w in range(3)]]
        bias = sb("bias", [P, 2, H])
        cols = sb("cols", [P, 2, KC])
        a1, b1 = kept["a1"], kept["b1"]
        ident = kept["ident"]
        after = sb("after", [P, P])
        num = kept["num"]

        xin = kept["xin"]
        xres = kept["xres"]
        adj_n = [sb(f"adj_n{s}", [P, G, S]) for s in (A, B)]
        adj_tr = [sb(f"adj_tr{s}", [P, G, S]) for s in (A, B)]
        m_left = [sb(f"m_left{s}", [P, G, S]) for s in (A, B)]
        m_right = [sb(f"m_right{s}", [P, G, S]) for s in (A, B)]
        ht = [kept["ht"], sb("ht_b", [P, KC, GS])]
        ht_hi = [kept["ht_hi"], sb("ht_hi_b", [P, KC, GS], F32R)]
        ht_lo = [kept["ht_lo"], sb("ht_lo_b", [P, KC, GS], F32R)]
        pt_hi = sb("pt_hi", [P, KC, 2, GS], F32R)
        pt_lo = sb("pt_lo", [P, KC, 2, GS], F32R)
        val = sb("val", [P, G, H])
        val_hi = sb("val_hi", [P, G, HV], F32R)
        val_lo = sb("val_lo", [P, G, HV], F32R)
        um = sb("um", [P, 2, G, S])
        eu = sb("eu", [P, G, S])
        eu_hi = sb("eu_hi", [P, G, S], F32R)
        eu_lo = sb("eu_lo", [P, G, S], F32R)
        c = [sb("c_a", [P, G, HV]), kept["c"]]
        rsum = [sb("rsum_a", [P, 2, G]), kept["rsum"]]
        stats = [sb(f"stats{s}", [P, G, 6]) for s in (A, B, FRONT)]
        mv = [sb(f"mv{s}", [P, G, 2]) for s in (A, B, FRONT)]
        inv = [sb(f"inv{s}", [P, 4, G]) for s in (A, B, FRONT)]

        staging = [b[:, 0:KC, 0:H] for b in (val, c[A], xres, ht[B], c[B], xres)]
        l1_staging = [b[:, 0:KC, 0:H] for b in (xin, c[A], xin)]

        pp = [ctx.enter_context(nc.psum_tensor(f"pp{i}", [P, 512], F32)) for i in range(3)]
        pq = [ctx.enter_context(nc.psum_tensor(f"pq{i}", [P, 512], F32)) for i in range(5)]
        p_full, p_empty = sems("p_full", 3), sems("p_empty", 3)
        q_full, q_empty = sems("q_full", 5), sems("q_empty", 5)

        ident_zero, ident_ready = sem("ident_zero"), sem("ident_ready")
        consts_loaded = sem("consts_loaded")
        consts_set = sem("consts_set")
        w_loaded, w_hi_ready, w_ready = sems("w_loaded", 9), sem("w_hi_ready"), sem("w_ready")
        l1_consts_loaded = sem("l1_consts_loaded")
        x_loaded, xres_loaded, x2_stored = sem("x_loaded"), sem("xres_loaded"), kept["x2_stored"]
        adj_loaded = sems("adj_loaded")
        masks_ready = sems("masks_ready")
        z_ready = sems("z_ready")
        ht_lo_ready = sems("ht_lo_ready")
        pt_hi_ready = sems("pt_hi_ready")
        val_hi_ready, val_lo_ready = sems("val_hi_ready"), sems("val_lo_ready")
        scores_summed, exp_ready = sems("scores_summed"), sems("exp_ready")
        e_ready, e_hi_ready, e_lo_ready = sems("e_ready"), sems("e_hi_ready"), sems("e_lo_ready")
        rsum_eps, rsum_ready, c_scaled = sems("rsum_eps"), sems("rsum_ready"), sems("c_scaled")
        bn_ready, mv_ready = sems("bn_ready", 3), sems("mv_ready", 3)
        inv_step, inv_ready = sems("inv_step", 3), sems("inv_ready", 3)
        out_centred, out_scaled, out_shifted = sem("out_centred"), sem("out_scaled"), sem("out_shifted")
        x2_ready = sem("x2_ready")

        x_g = x.rearrange("(g b) s h -> g s b h", b=G)
        x2_g = x2.rearrange("(g b) s h -> g s b h", b=G)
        adj_g = adj.rearrange("(g b) i j -> g i b j", b=G)
        adj_t_g = adj_t.rearrange("(g b) j i -> g j b i", b=G)

        def jobs(t, a, b, n, f):
            order_p, order_q = [], []
            if a:
                order_p += [("pt", A, j) for j in range(2 * KC)]
            if f:
                order_q += [("ctx", B, i) for i in range(G)]
            if b:
                order_p += [("ht", B, k) for k in range(KC)]
            if a:
                order_q += [("val", A, 0), ("val", A, 1), ("u", A, 0), ("u", A, 1), ("val", A, 2), ("val", A, 3)]
            if b:
                order_p += [("pt", B, j) for j in range(2 * KC)]
            if a:
                order_q += [("ctx", A, i) for i in range(G)]
            if b:
                order_q += [("u", B, 0), ("u", B, 1)] + [("val", B, i) for i in range(G)]
            if n:
                order_p += [("ht", A, k) for k in range(KC)]
            if isinstance(t, int):
                n_a, n_b = min(t, groups) if t > 0 else 0, max(0, min(t - 1, groups))
                n_n, n_f = min(t + 1, groups + 1), max(0, t - 2)
                rounds_q, extra_q = divmod(10 * n_a + 6 * n_b + 4 * n_f, 5)
                return {**psum_jobs(order_p, 3, 2 * n_a + 3 * n_b + n_n),
                        **psum_jobs(order_q, 5, rounds_q, extra_q)}
            return {**psum_jobs(order_p, 3, 6 * t - 2), **psum_jobs(order_q, 5, 4 * t - 3, 1)}

        def bank_of(job, table):
            ring = (pp, p_full, p_empty) if job[0] in ("ht", "pt") else (pq, q_full, q_empty)
            n, use = table[job]
            return ring[0][n], ring[1][n], ring[2][n], use

        def run(engine, iteration):
            def flags(t):
                return 0 <= t < groups, 1 <= t <= groups, -1 <= t < groups, 2 <= t <= groups + 1
            for t in range(-1, 3):
                iteration(t, *flags(t))
            with engine.Fori(3, groups - 1) as t:
                iteration(t, True, True, True, True)
            for t in range(groups - 1, groups + 2):
                iteration(t, *flags(t))

        block = ctx.enter_context(nc.Block())

        @block.sync
        def _(sp):
            def load_x(src):
                sp.dma_start(xin[:], src).then_inc(x_loaded, 16)

            def load_adj(s, g):
                sp.dma_start(adj_tr[s][:], adj_t_g[g]).then_inc(adj_loaded[s], 16)
                sp.dma_start(adj_n[s][:], adj_g[g]).then_inc(adj_loaded[s], 16)

            def load_weights(s, w):
                src = (w_left, w_right, w_lin_t)[w][s].rearrange("(k p) n -> p k n", p=P)
                sp.dma_start(staging[3 * s + w], src).then_inc(w_loaded[3 * s + w], 16)

            def load_l1_weights(w):
                src = l1_weights[w].rearrange("(k p) n -> p k n", p=P)
                sp.dma_start(l1_staging[w], src).then_inc(w_loaded[6 + w], 16)

            load_x(x_g[0])
            for w in range(3):
                load_weights(A, w)
            sp.dma_start(cols[:], ln_cols).then_inc(consts_loaded, 16)
            sp.dma_start(bias[:], b_lin.partition_broadcast(P)).then_inc(consts_loaded, 16)
            sp.dma_start(a1[:], ln_a1.partition_broadcast(P)).then_inc(consts_loaded, 16)
            sp.dma_start(b1[:], ln_b1.partition_broadcast(P)).then_inc(consts_loaded, 16)
            load_weights(B, 0)
            load_weights(B, 1)

            def iteration(t, a, b, n, f):
                if n and not is_step(t, -1):
                    sp.wait_ge(ht_lo_ready[A], KC * (t + 1))
                    load_x(x2_g[0] if is_step(t, groups - 1) else x_g[t + 1])
                if a:
                    if not isinstance(t, int) or t >= 1:
                        sp.wait_ge(e_ready[A], t)
                    load_adj(A, t)
                    if is_step(t, 0):
                        sp.wait_ge(w_ready, 3)
                        load_weights(B, 2)
                if b:
                    if not isinstance(t, int) or t >= 2:
                        sp.wait_ge(e_ready[B], t - 1)
                    load_adj(B, t - 1)
                if is_step(t, 2):
                    for buf, src in zip(kept["l1_consts"], l1_consts):
                        sp.dma_start(buf[:], src.partition_broadcast(P)).then_inc(l1_consts_loaded, 16)
                if is_step(t, groups):
                    sp.wait_ge(ht_lo_ready[A], KC * (groups + 1))
                    load_l1_weights(0)
                    sp.wait_ge(ht_lo_ready[B], KC * groups)
                    load_l1_weights(1)
                    sp.wait_ge(w_ready, 7)
                    load_l1_weights(2)
                if f and not is_step(t, groups + 1):
                    sp.wait_ge(x2_ready, t - 1)
                    sp.dma_start(x2_g[t - 2], xres[:]).then_inc(x2_stored, 16)
                    if not is_step(t, groups):
                        sp.wait_ge(x2_stored, 16 * (t - 1))
                if b and not is_step(t, groups):
                    if is_step(t, 1):
                        sp.wait_ge(w_ready, 6)
                    sp.dma_start(xres[:], x_g[t - 1]).then_inc(xres_loaded, 16)

            run(sp, iteration)
            sp.wait_ge(l1_consts_loaded, 16 * len(l1_consts))

        @block.tensor
        def _(pe):
            def open_bank(job, table):
                bank, full, empty, use = bank_of(job, table)
                if not isinstance(use, int) or use > 1:
                    pe.wait_ge(empty, use - 1)
                return bank, full

            def transposes(s, table, src):
                for k in range(KC):
                    bank, full = open_bank(("ht", s, k), table)
                    for i in range(G):
                        mm = pe.transpose(bank[:, i * S:(i + 1) * S], src[:, i, k * P:(k + 1) * P], ident[:])
                    mm.then_inc(full, 1)

            def split_product(out, pairs):
                last = len(pairs) - 1
                for n, ((l_hi, l_lo), (r_hi, r_lo)) in enumerate(pairs):
                    pe.matmul(out, l_hi, r_hi, start=(n == 0), stop=False)
                    pe.matmul(out, l_hi, r_lo, start=False, stop=False)
                    mm = pe.matmul(out, l_lo, r_hi, start=False, stop=(n == last))
                return mm

            def project(s, table):
                for j in range(2 * KC):
                    m, w = j // 2, j % 2
                    bank, full = open_bank(("pt", s, j), table)
                    cut = slice(m * P, (m + 1) * P)
                    split_product(bank[:], [
                        ((w_hi[s][w][:, k, cut], w_lo[s][w][:, k, cut]), (ht_hi[s][:, k, :], ht_lo[s][:, k, :]))
                        for k in range(KC)]).then_inc(full, 1)

            def values(s, graphs, table):
                for i in graphs:
                    bank, full = open_bank(("val", s, i), table)
                    cut = slice(i * S, (i + 1) * S)
                    split_product(bank[:, 0:H], [
                        ((ht_hi[s][:, k, cut], ht_lo[s][:, k, cut]), (w_hi[s][2][:, k, :], w_lo[s][2][:, k, :]))
                        for k in range(KC)]).then_inc(full, 1)

            def scores(s, table):
                for half in range(2):
                    bank, full = open_bank(("u", s, half), table)
                    for i in (2 * half, 2 * half + 1):
                        cut = slice(i * S, (i + 1) * S)
                        at = (i % 2) * 2 * S
                        mm = split_product(bank[:, at:at + 2 * S].rearrange("p (w i) -> p w i", w=2), [
                            ((ht_hi[s][:, k, cut], ht_lo[s][:, k, cut]), (pt_hi[:, k, :, cut], pt_lo[:, k, :, cut]))
                            for k in range(KC)])
                    mm.then_inc(full, 1)

            def context(s, g, table):
                pe.wait_ge(e_lo_ready[s], g + 1)
                for i in range(G):
                    pe.wait_ge(val_lo_ready[s], G * g + i + 1)
                    bank, full = open_bank(("ctx", s, i), table)
                    split_product(bank[:, 0:HV], [
                        ((eu_hi[:, i, :], eu_lo[:, i, :]), (val_hi[:, i, :], val_lo[:, i, :]))]).then_inc(full, 1)

            pe.wait_ge(ident_ready, 1)

            def iteration(t, a, b, n, f):
                table = jobs(t, a, b, n, f)
                fill = is_step(t, 0)
                drain = is_step(t, groups)
                if is_step(t, 0):
                    pe.wait_ge(w_ready, 2)
                if is_step(t, 1):
                    pe.wait_ge(w_ready, 5)
                if a:
                    pe.wait_ge(ht_lo_ready[A], KC * (t + 1))
                    project(A, table)
                if f and not drain:
                    context(B, t - 2, table)
                if b:
                    pe.wait_ge(z_ready[B], t)
                    transposes(B, table, c[A])
                if f and drain:
                    context(B, t - 2, table)
                if a:
                    if is_step(t, 0):
                        pe.wait_ge(w_ready, 3)
                    values(A, (0, 1), table)
                    _, _, empty, use = bank_of(("pt", A, 2 * KC - 1), table)
                    pe.wait_ge(empty, use)
                    scores(A, table)
                    values(A, (2, 3), table)
                if b:
                    pe.wait_ge(ht_lo_ready[B], KC * t)
                    project(B, table)
                if n and fill:
                    pe.wait_ge(z_ready[A], t + 2)
                    transposes(A, table, xin)
                if a:
                    context(A, t, table)
                if b:
                    _, _, empty, use = bank_of(("pt", B, 2 * KC - 1), table)
                    pe.wait_ge(empty, use)
                    scores(B, table)
                    if is_step(t, 1):
                        pe.wait_ge(w_ready, 6)
                    values(B, (0,), table)
                if n and not fill:
                    pe.wait_ge(z_ready[A], t + 2)
                    transposes(A, table, xin)
                if b:
                    values(B, (1, 2, 3), table)

            run(pe, iteration)

        @block.scalar
        def _(act):
            def turned(s, table):
                for k in range(KC):
                    bank, full, empty, use = bank_of(("ht", s, k), table)
                    act.wait_ge(full, use)
                    affine = {} if s == A else {"scale": cols[:, 0, k:k + 1], "bias": cols[:, 1, k:k + 1]}
                    act.activation(ht_hi[s][:, k, :], bank[:], ACT.Relu, **affine)
                    act.activation(ht[s][:, k, :], bank[:], ACT.Relu, **affine).then_inc(empty, 1)

            def pt_high(s, js, table):
                for j in js:
                    bank, full, _, use = bank_of(("pt", s, j), table)
                    act.wait_ge(full, use)
                    act.copy(pt_hi[:, j // 2, j % 2, :], bank[:]).then_inc(pt_hi_ready[s], 1)

            def val_high(s, graphs, table):
                for i in graphs:
                    _, _, empty, use = bank_of(("val", s, i), table)
                    act.wait_ge(empty, use)
                    act.copy(val_hi[:, i, 0:H], val[:, i, :]).then_inc(val_hi_ready[s], 1)

            def exponential(s, g):
                act.wait_ge(scores_summed[s], g + 1)
                act.activation(eu[:], eu[:], ACT.Exp, scale=1.0 / TEMPER).then_inc(exp_ready[s], 1)

            def e_high(s, g):
                act.wait_ge(e_ready[s], g + 1)
                act.copy(eu_hi[:], eu[:]).then_inc(e_hi_ready[s], 1)

            def context_out(s, table):
                for i in range(G):
                    bank, full, empty, use = bank_of(("ctx", s, i), table)
                    act.wait_ge(full, use)
                    act.copy(c[s][:, i, :], bank[:, 0:HV]).then_inc(empty, 1)

            def context_scale(s, g, table):
                _, _, empty, use = bank_of(("ctx", s, G - 1), table)
                act.wait_ge(empty, use)
                act.wait_ge(rsum_ready[s], g + 1)
                for i in range(G):
                    act.activation(c[s][:, i, 0:H], c[s][:, i, 0:H], ACT.Copy,
                                   scale=rsum[s][:, 1, i:i + 1]).then_inc(c_scaled[s], 1)

            def weights_high(n, w_hi, staged):
                act.wait_ge(w_loaded[n], 16)
                act.copy(w_hi[:], staged).then_inc(w_hi_ready, 1)

            for w in range(3):
                weights_high(w, w_hi[A][w], staging[w])

            def iteration(t, a, b, n, f):
                table = jobs(t, a, b, n, f)
                fill = is_step(t, 0)
                drain = is_step(t, groups)
                if is_step(t, 1):
                    act.wait_ge(consts_loaded, 4 * 16)
                if a:
                    pt_high(A, range(2 * KC), table)
                if fill:
                    for w in range(3):
                        weights_high(3 + w, w_hi[B][w], staging[3 + w])
                if b and drain:
                    turned(B, table)
                if f:
                    if not isinstance(t, int) or t >= 3:
                        act.wait_ge(x2_ready, t - 2)
                    context_out(B, table)
                if b and not drain:
                    turned(B, table)
                if f and not is_step(t, groups + 1):
                    context_scale(B, t - 2, table)
                if a:
                    val_high(A, (0, 1, 2), table)
                    exponential(A, t)
                    val_high(A, (3,), table)
                if b:
                    pt_high(B, range(0, 2), table)
                if a:
                    e_high(A, t)
                if b:
                    pt_high(B, (2,), table)
                if drain:
                    _, last_values, _, use = bank_of(("val", A, G - 1), jobs(groups - 1, True, True, True, True))
                    act.wait_ge(last_values, use)
                    weights_high(6, w_hi[A][0], l1_staging[0])
                if b:
                    pt_high(B, range(3, 2 * KC), table)
                if drain:
                    weights_high(7, w_hi[A][1], l1_staging[1])
                    weights_high(8, w_hi[A][2], l1_staging[2])
                if n and fill:
                    turned(A, table)
                if a:
                    context_out(A, table)
                    context_scale(A, t, table)
                if b:
                    val_high(B, (0,), table)
                if n and not fill:
                    turned(A, table)
                if b:
                    exponential(B, t - 1)
                    val_high(B, (1,), table)
                    e_high(B, t - 1)
                    val_high(B, (2, 3), table)

            run(act, iteration)

        @block.vector
        def _(dve):
            def moments(s, g, src, step):
                for i in range(G):
                    if step is not None:
                        dve.wait_ge(step, G * g + i + 1)
                    bn = dve.bn_stats(stats[s][:, i, :], src[:, i, 0:H])
                bn.then_inc(bn_ready[s], 1)
                dve.wait_ge(consts_set, 1)
                dve.wait_ge(bn_ready[s], g + 1)
                for i in range(G):
                    ag = dve.bn_aggr(mv[s][:, i, :], stats[s][:, i, :])
                ag.then_inc(mv_ready[s], 1)

            def centre(s, g, src):
                dve.wait_ge(inv_ready[s], g + 1)
                for i in range(G):
                    z = dve.tensor_scalar(src[:, i, 0:H], src[:, i, 0:H], mv[s][:, i, 0:1],
                                          inv[s][:, 3, i:i + 1], ALU.subtract, ALU.mult)
                return z

            def turned_low(s, table):
                for k in range(KC):
                    _, _, empty, use = bank_of(("ht", s, k), table)
                    dve.wait_ge(empty, use)
                    dve.tensor_tensor(ht_lo[s][:, k, :], ht[s][:, k, :], ht_hi[s][:, k, :].bitcast(F32),
                                      ALU.subtract).then_inc(ht_lo_ready[s], 1)

            def pt_low(s, g, js, table):
                for j in js:
                    bank, _, empty, use = bank_of(("pt", s, j), table)
                    dve.wait_ge(pt_hi_ready[s], 2 * KC * g + j + 1)
                    dve.tensor_tensor(pt_lo[:, j // 2, j % 2, :], bank[:], pt_hi[:, j // 2, j % 2, :].bitcast(F32),
                                      ALU.subtract).then_inc(empty, 1)

            def values_out(s, graphs, table, free, free_count):
                for i in graphs:
                    bank, full, empty, use = bank_of(("val", s, i), table)
                    dve.wait_ge(full, use)
                    if free is not None:
                        dve.wait_ge(free, free_count + i)
                    dve.tensor_tensor(val[:, i, :], bank[:, 0:H], bias[:, s, :], ALU.add).then_inc(empty, 1)

            def masked(s, g, table):
                dve.wait_ge(masks_ready[s], g + 1)
                for half in range(2):
                    bank, full, empty, use = bank_of(("u", s, half), table)
                    dve.wait_ge(full, use)
                    two = slice(2 * half, 2 * half + 2)
                    u = bank[:].rearrange("p (b w i) -> p b w i", b=2, w=2)
                    dve.tensor_tensor(um[:, 0, two, :], u[:, :, 0, :], m_left[s][:, two, :], ALU.mult)
                    dve.tensor_tensor(um[:, 1, two, :], u[:, :, 1, :], m_right[s][:, two, :],
                                      ALU.mult).then_inc(empty, 1)

            def e_low(s, g):
                dve.wait_ge(e_hi_ready[s], g + 1)
                dve.tensor_tensor(eu_lo[:], eu[:], eu_hi[:].bitcast(F32), ALU.subtract).then_inc(e_lo_ready[s], 1)

            def inverse_sums(s, g, table):
                _, _, empty, use = bank_of(("ctx", s, G - 1), table)
                dve.wait_ge(empty, use)
                dve.tensor_scalar(rsum[s][:, 0, :], c[s][:, :, H], SUM_EPS, None, ALU.add).then_inc(rsum_eps[s], 1)
                dve.wait_ge(rsum_eps[s], g + 1)
                dve.reciprocal(rsum[s][:, 1, :], rsum[s][:, 0, :]).then_inc(rsum_ready[s], 1)

            for n, number in enumerate(NUMBERS):
                dve.memset(num[:, n, :], number)
            dve.memset(val_hi[:, :, H:H + 1].bitcast(F32), 1.0)
            dve.memset(val_hi[:, :, H + 1:HV].bitcast(F32), 0.0)
            dve.memset(val_lo[:, :, H:HV].bitcast(F32), 0.0).then_inc(consts_set, 1)

            def front(g):
                dve.wait_ge(x_loaded, 16 * (g + 1))
                moments(FRONT, g, xin, None)

            def weights_low(n, w_hi, w_lo, staged):
                dve.wait_ge(w_loaded[n], 16)
                dve.wait_ge(w_hi_ready, n + 1)
                dve.tensor_tensor(w_lo[:], staged, w_hi[:].bitcast(F32), ALU.subtract).then_inc(w_ready, 1)

            def l0_weights_low(s, w):
                weights_low(3 * s + w, w_hi[s][w], w_lo[s][w], staging[3 * s + w])

            def l1_weights_low(w):
                weights_low(6 + w, w_hi[A][w], w_lo[A][w], l1_staging[w])

            def fill_first():
                front(0)
                l0_weights_low(A, 0)
                centre(FRONT, 0, xin).then_inc(z_ready[A], 1)
                l0_weights_low(A, 1)
                turned_low(A, jobs(-1, False, False, True, False))
                l0_weights_low(A, 2)

            def fill_second():
                table = jobs(0, True, False, True, False)
                pt_low(A, 0, range(0, 2), table)
                front(1)
                pt_low(A, 0, range(2, 2 * KC), table)
                dve.wait_ge(consts_loaded, 4 * 16)
                centre(FRONT, 1, xin).then_inc(z_ready[A], 1)
                values_out(A, (0, 1), table, None, 0)
                masked(A, 0, table)
                values_out(A, (2, 3), table, None, 0)
                l0_weights_low(B, 0)
                e_low(A, 0)
                l0_weights_low(B, 1)
                turned_low(A, table)
                inverse_sums(A, 0, table)
                l0_weights_low(B, 2)
                moments(A, 0, c[A], c_scaled[A])

            def iteration(t, a, b, n, f):
                table = jobs(t, a, b, n, f)
                tail = is_step(t, groups + 1)
                last_a = is_step(t, groups - 1)
                drain = is_step(t, groups)
                if is_step(t, -1):
                    fill_first()
                    return
                if is_step(t, 0):
                    fill_second()
                    return
                if a:
                    pt_low(A, t, range(0, 2), table)
                if b and not drain:
                    centre(A, t - 1, c[A]).then_inc(z_ready[B], 1)
                if a:
                    pt_low(A, t, range(2, 2 * KC), table)
                if b and drain:
                    turned_low(B, table)
                if f:
                    inverse_sums(B, t - 2, table)
                if b and not drain:
                    turned_low(B, table)
                if f and not tail:
                    moments(B, t - 2, c[B], c_scaled[B])
                free = (val_lo_ready[B], G * (t - 2) + 1) if not isinstance(t, int) or t >= 2 else (None, 0)
                if a:
                    values_out(A, (0, 1), table, *free)
                    masked(A, t, table)
                    values_out(A, (2, 3), table, *free)
                if n:
                    front(t + 1)
                if b:
                    pt_low(B, t - 1, range(0, 2), table)
                if f and not tail:
                    centre(B, t - 2, c[B]).then_inc(out_centred, 1)
                if b:
                    pt_low(B, t - 1, range(2, 3), table)
                if a:
                    e_low(A, t)
                if drain:
                    l1_weights_low(0)
                if b:
                    pt_low(B, t - 1, range(3, 2 * KC), table)
                if drain:
                    l1_weights_low(1)
                    l1_weights_low(2)
                if n:
                    centre(FRONT, t + 1, xin).then_inc(z_ready[A], 1)
                if a:
                    inverse_sums(A, t, table)
                    moments(A, t, c[A], c_scaled[A])
                free = (val_lo_ready[A], G * (groups - 1 if drain else t) + 1)
                if b:
                    masked(B, t - 1, table)
                    values_out(B, (0,), table, *free)
                if n:
                    turned_low(A, table)
                if b:
                    values_out(B, (1, 2, 3), table, *free)
                if last_a:
                    centre(A, t, c[A]).then_inc(z_ready[B], 1)
                if b:
                    e_low(B, t - 1)
                if f and not tail:
                    dve.wait_ge(out_shifted, t - 1)
                    dve.wait_ge(xres_loaded, 16 * (t - 1))
                    dve.scalar_tensor_tensor(xres[:], c[B][:, :, 0:H], 0.0, xres[:], ALU.max,
                                             ALU.add).then_inc(x2_ready, 1)
            run(dve, iteration)

        @block.gpsimd
        def _(pool):
            pool.memset(ident[:], 0.0).then_inc(ident_zero, 1)
            pool.wait_ge(ident_zero, 1)
            pool.affine_select(out=ident[:], in_=ident[:], compare_op=ALU.not_equal, fill=1.0, base=0,
                               pattern=[[-1, P]], channel_multiplier=1).then_inc(ident_ready, 1)
            pool.memset(after[:], 1.0).then_inc(ident_zero, 1)
            pool.wait_ge(ident_zero, 2)
            pool.affine_select(out=after[:], in_=after[:], compare_op=ALU.is_gt, fill=0.0, base=0,
                               pattern=[[1, P]], channel_multiplier=-1).then_inc(ident_ready, 1)
            pool.wait_ge(ident_ready, 2)
            pool.wait_ge(consts_set, 1)

            def masks(s, g):
                pool.wait_ge(adj_loaded[s], 32 * (g + 1))
                pool.tensor_tensor(m_right[s][:], adj_n[s][:], after[:, None, :].to_broadcast([P, G, S]), ALU.mult)
                pool.affine_select(out=m_left[s][:], in_=adj_tr[s][:], compare_op=ALU.is_ge, fill=0.0, base=0,
                                   pattern=[[0, G], [-1, S]], channel_multiplier=1).then_inc(masks_ready[s], 1)

            def front_inverse(g):
                pool.wait_ge(mv_ready[FRONT], g + 1)
                pool.tensor_tensor(inv[FRONT][:, 0, :], mv[FRONT][:, :, 1], num[:, N_LN_EPS, :],
                                   ALU.add).then_inc(inv_step[FRONT], 1)
                pool.wait_ge(inv_step[FRONT], g + 1)
                pool.tensor_tensor(inv[FRONT][:, 3, :], inv[FRONT][:, 0, :], num[:, RSQRT, :],
                                   ALU.pow).then_inc(inv_ready[FRONT], 1)

            def sigma_inverse(s, g):
                pool.wait_ge(mv_ready[s], g + 1)
                pool.tensor_tensor(inv[s][:, 0, :], mv[s][:, :, 1], num[:, N_UNBIAS, :],
                                   ALU.mult).then_inc(inv_step[s], 1)
                pool.wait_ge(inv_step[s], 3 * g + 1)
                pool.tensor_tensor(inv[s][:, 1, :], inv[s][:, 0, :], num[:, SQRT, :],
                                   ALU.pow).then_inc(inv_step[s], 1)
                pool.wait_ge(inv_step[s], 3 * g + 2)
                pool.tensor_tensor(inv[s][:, 2, :], inv[s][:, 1, :], num[:, N_L0_EPS, :],
                                   ALU.add).then_inc(inv_step[s], 1)
                pool.wait_ge(inv_step[s], 3 * g + 3)
                pool.tensor_tensor(inv[s][:, 3, :], inv[s][:, 2, :], num[:, MINUS_ONE, :],
                                   ALU.pow).then_inc(inv_ready[s], 1)

            def values_low(s, g, graphs):
                for i in graphs:
                    pool.wait_ge(val_hi_ready[s], G * g + i + 1)
                    pool.tensor_tensor(val_lo[:, i, 0:H], val[:, i, :], val_hi[:, i, 0:H].bitcast(F32),
                                       ALU.subtract).then_inc(val_lo_ready[s], 1)

            def sum_scores(s, g, table):
                _, _, empty, use = bank_of(("u", s, 1), table)
                pool.wait_ge(empty, use)
                pool.tensor_tensor(eu[:], um[:, 0], um[:, 1], ALU.add).then_inc(scores_summed[s], 1)

            def mask_exp(s, g):
                pool.wait_ge(exp_ready[s], g + 1)
                pool.tensor_tensor(eu[:], eu[:], adj_tr[s][:], ALU.mult).then_inc(e_ready[s], 1)

            def end_affine(g):
                pool.wait_ge(out_centred, g + 1)
                pool.tensor_tensor(c[B][:, :, 0:H], c[B][:, :, 0:H], a1[:, None, :].to_broadcast([P, G, H]),
                                   ALU.mult).then_inc(out_scaled, 1)
                pool.wait_ge(out_scaled, g + 1)
                pool.tensor_tensor(c[B][:, :, 0:H], c[B][:, :, 0:H], b1[:, None, :].to_broadcast([P, G, H]),
                                   ALU.add).then_inc(out_shifted, 1)

            def iteration(t, a, b, n, f):
                table = jobs(t, a, b, n, f)
                fill = is_step(t, 0)
                last_a = is_step(t, groups - 1)
                drain = is_step(t, groups)
                tail = is_step(t, groups + 1)
                if drain:
                    sigma_inverse(B, t - 2)
                if a:
                    masks(A, t)
                if b:
                    masks(B, t - 1)
                if n and fill:
                    front_inverse(t + 1)
                if a:
                    values_low(A, t, (0, 1))
                    sum_scores(A, t, table)
                if f and not tail and not drain:
                    sigma_inverse(B, t - 2)
                if a:
                    values_low(A, t, (2,))
                    mask_exp(A, t)
                    values_low(A, t, (3,))
                if n and not fill:
                    front_inverse(t + 1)
                if f and not tail:
                    end_affine(t - 2)
                if b:
                    sum_scores(B, t - 1, table)
                    values_low(B, t - 1, (0,))
                if last_a:
                    sigma_inverse(A, t)
                if b:
                    mask_exp(B, t - 1)
                    values_low(B, t - 1, (1, 2, 3))
                if a and not last_a:
                    sigma_inverse(A, t)

            run(pool, iteration)


def l1_phase(nc, kept, x, x2, adj_t, out):
    n_graphs, S, H = x2.shape
    groups = n_graphs // G
    KC = H // P
    GS = G * S
    HV = H + 2
    SUM_EPS = 1e-10
    SCALE = 1.0 / float(H) ** 0.5
    END, TAIL = 0, 1
    LEFT, RIGHT, SELF = 0, 1, 2

    with ExitStack() as ctx:
        def sb(name, shape, dt=F32):
            return ctx.enter_context(nc.sbuf_tensor("l1_" + name, shape, dt))

        def sem(name):
            return ctx.enter_context(nc.semaphore("l1_" + name))

        def sems(name, n=2):
            return [sem(f"{name}{i}") for i in range(n)]

        w_hi, w_lo, ident, xin = kept["w_hi"], kept["w_lo"], kept["ident"], kept["xin"]
        ht, ht_hi, ht_lo = kept["ht"], kept["ht_hi"], kept["ht_lo"]
        bias, gam, bet = kept["l1_consts"]
        num = kept["num"]
        tail_x, tail_c, tail_rsum, a1, b1 = kept["xres"], kept["c"], kept["rsum"], kept["a1"], kept["b1"]
        xres = sb("xres", [P, G, H])
        adj_tr = sb("adj_tr", [P, G, S])
        m_lr = sb("m_lr", [P, 2, G, S])
        m_self = sb("m_self", [P, G, S])
        val = [sb(f"val{w}", [P, G, H]) for w in (LEFT, RIGHT)]
        val_hi = [sb(f"val_hi{w}", [P, G, HV], F32R) for w in (LEFT, RIGHT)]
        val_lo = [sb(f"val_lo{w}", [P, G, HV], F32R) for w in (LEFT, RIGHT)]
        own = sb("own", [P, G, HV])
        neg_max = sb("neg_max", [P, 2, G])
        e = sb("e", [P, G, S])
        e_diag = sb("e_diag", [P, G, S])
        z_sum = sb("z_sum", [P, G])
        diag = sb("diag", [P, G])
        et = sb("et", [P, 2, G, S])
        et_hi = sb("et_hi", [P, 2, G, S], F32R)
        et_lo = sb("et_lo", [P, 2, G, S], F32R)
        c = sb("c", [P, G, HV])
        zc = sb("zc", [P, G, H])
        q = sb("q", [P, 4, G])
        stats = [sb(f"stats{n}", [P, G, 6]) for n in (END, TAIL, FRONT)]
        mv = [sb(f"mv{n}", [P, G, 2]) for n in (END, TAIL, FRONT)]
        inv = [sb(f"inv{n}", [P, 4, G]) for n in (END, TAIL, FRONT)]

        ps = [ctx.enter_context(nc.psum_tensor("l1_ps", [P, 512], F32))]
        pp = [ctx.enter_context(nc.psum_tensor(f"l1_pp{i}", [P, 512], F32)) for i in range(KC)]
        pq = [ctx.enter_context(nc.psum_tensor(f"l1_pq{i}", [P, 512], F32)) for i in range(G)]
        s_full, s_empty = sems("s_full", 1), sems("s_empty", 1)
        p_full, p_empty = sems("p_full", KC), sems("p_empty", KC)
        q_full, q_empty = sems("q_full", G), sems("q_empty", G)

        consts_set = sem("consts_set")
        x_loaded, xres_loaded, adj_loaded = sem("x_loaded"), sem("xres_loaded"), sem("adj_loaded")
        masks_ready = sem("masks_ready")
        bn_ready, mv_ready = sems("bn_ready", 3), sems("mv_ready", 3)
        inv_step, inv_ready = sems("inv_step", 3), sems("inv_ready", 3)
        z_ready, ht_ready = sems("z_ready", 3), sem("ht_ready")
        max_ready, bias_ready = sem("max_ready"), sem("bias_ready")
        diag_masked, diag_ready = sem("diag_masked"), sem("diag_ready")
        et_hi_ready, et_lo_ready = sem("et_hi_ready"), sem("et_lo_ready")
        val_hi_ready, val_lo_ready = sem("val_hi_ready"), sem("val_lo_ready")
        q_ready = sem("q_ready")
        tail_divided, tail_centred = sem("tail_divided"), sem("tail_centred")
        tail_scaled, tail_shifted = sem("tail_scaled"), sem("tail_shifted")
        tail_loaded, tail_ready, tail_stored = sem("tail_loaded"), sem("tail_ready"), sem("tail_stored")
        scaled, shifted, out_ready, out_stored = sem("scaled"), sem("shifted"), sem("out_ready"), sem("out_stored")

        x_g = x2.rearrange("(g b) s h -> g s b h", b=G)
        tail_src = x.rearrange("(g b) s h -> g s b h", b=G)[groups - 1]
        out_g = out.rearrange("(g b) s h -> g s b h", b=G)
        adj_t_g = adj_t.rearrange("(g b) j i -> g j b i", b=G)

        def jobs(t, a, n):
            table = {}
            if n:
                table |= psum_jobs([("ht", k) for k in range(KC)], KC, t)
            if a:
                table |= psum_jobs([("u", 0), ("et", 0)], 1, 2 * t)
                table |= psum_jobs([("val", w, i) for w in (LEFT, RIGHT, SELF) for i in range(G)] +
                                   [("ctx", i) for i in range(G)], G, 4 * t)
            return table

        def bank_of(job, table):
            if job[0] in ("u", "et"):
                ring = (ps, s_full, s_empty)
            elif job[0] == "ht":
                ring = (pp, p_full, p_empty)
            else:
                ring = (pq, q_full, q_empty)
            n, use = table[job]
            return ring[0][n], ring[1][n], ring[2][n], use

        def affine(engine, done):
            engine.wait_ge(z_ready[END], done)
            engine.tensor_tensor(zc[:], zc[:], gam[:, None, :].to_broadcast([P, G, H]), ALU.mult).then_inc(scaled, 1)
            engine.wait_ge(scaled, done)
            engine.tensor_tensor(zc[:], zc[:], bet[:, None, :].to_broadcast([P, G, H]), ALU.add).then_inc(shifted, 1)

        def run(engine, iteration):
            iteration(0, True, True, False, False)
            iteration(1, True, True, True, False)
            iteration(2, True, True, True, True)
            with engine.Fori(3, groups - 1) as t:
                iteration(t, True, True, True, True)
            iteration(groups - 1, True, False, True, True)
            iteration(groups, False, False, True, True)
            iteration(groups + 1, False, False, False, True)

        block = ctx.enter_context(nc.Block())

        @block.sync
        def _(sp):
            def iteration(t, a, n, f, o):
                if n:
                    if not isinstance(t, int) or t >= 1:
                        sp.wait_ge(ht_ready, KC * t)
                    sp.dma_start(xin[:], x_g[t + 1]).then_inc(x_loaded, 16)
                if a:
                    if not isinstance(t, int) or t >= 1:
                        sp.wait_ge(masks_ready, t)
                    sp.dma_start(adj_tr[:], adj_t_g[t]).then_inc(adj_loaded, 16)
                if is_step(t, 0):
                    sp.wait_ge(kept["x2_stored"], 16 * (groups - 1))
                    sp.dma_start(tail_x[:], tail_src).then_inc(tail_loaded, 16)
                if is_step(t, 2):
                    sp.wait_ge(tail_ready, 1)
                    sp.dma_start(x_g[groups - 1], tail_x[:]).then_inc(tail_stored, 16)
                if o:
                    sp.wait_ge(out_ready, t - 1)
                    sp.dma_start(out_g[t - 2], xres[:]).then_inc(out_stored, 16)
                    sp.wait_ge(out_stored, 16 * (t - 1))
                if f:
                    sp.dma_start(xres[:], x_g[t - 1]).then_inc(xres_loaded, 16)
                if is_step(t, 2):
                    sp.wait_ge(tail_stored, 16)

            run(sp, iteration)

        @block.tensor
        def _(pe):
            def open_bank(job, table):
                bank, full, empty, use = bank_of(job, table)
                if not isinstance(use, int) or use > 1:
                    pe.wait_ge(empty, use - 1)
                return bank, full

            def split_product(out_ap, pairs):
                last = len(pairs) - 1
                for n, ((l_hi, l_lo), (r_hi, r_lo)) in enumerate(pairs):
                    pe.matmul(out_ap, l_hi, r_hi, start=(n == 0), stop=False)
                    pe.matmul(out_ap, l_hi, r_lo, start=False, stop=False)
                    mm = pe.matmul(out_ap, l_lo, r_hi, start=False, stop=(n == last))
                return mm

            def scores(table):
                bank, full = open_bank(("u", 0), table)
                for i in range(G):
                    cut = slice(i * S, (i + 1) * S)
                    for k in range(KC):
                        mm = pe.matmul(bank[:, cut], ht[:, k, cut], ht[:, k, cut], start=(k == 0), stop=(k == KC - 1))
                mm.then_inc(full, 1)

            def values(w, table):
                for i in range(G):
                    bank, full = open_bank(("val", w, i), table)
                    cut = slice(i * S, (i + 1) * S)
                    split_product(bank[:, 0:H], [
                        ((ht_hi[:, k, cut], ht_lo[:, k, cut]), (w_hi[w][:, k, :], w_lo[w][:, k, :]))
                        for k in range(KC)]).then_inc(full, 1)

            def iteration(t, a, n, f, o):
                table = jobs(t, a, n)
                if a:
                    if not isinstance(t, int) or t >= 1:
                        pe.wait_ge(ht_ready, KC * t)
                    scores(table)
                    values(LEFT, table)
                    bank, full = open_bank(("et", 0), table)
                    for i in range(G):
                        mm = pe.transpose(bank[:, i * S:(i + 1) * S], e[:, i, :], ident[:])
                    mm.then_inc(full, 1)
                    values(RIGHT, table)
                    values(SELF, table)
                if n:
                    pe.wait_ge(z_ready[FRONT], t + 1)
                    for k in range(KC):
                        bank, full = open_bank(("ht", k), table)
                        for i in range(G):
                            mm = pe.transpose(bank[:, i * S:(i + 1) * S], xin[:, i, k * P:(k + 1) * P], ident[:])
                        mm.then_inc(full, 1)
                if a:
                    pe.wait_ge(et_lo_ready, t + 1)
                    pe.wait_ge(val_lo_ready, 2 * G * (t + 1))
                    for i in range(G):
                        bank, full = open_bank(("ctx", i), table)
                        split_product(bank[:, 0:HV], [
                            ((et_hi[:, w, i, :], et_lo[:, w, i, :]), (val_hi[w][:, i, :], val_lo[w][:, i, :]))
                            for w in (LEFT, RIGHT)]).then_inc(full, 1)

            run(pe, iteration)

        @block.scalar
        def _(act):
            def values_high(w, t, table):
                for i in range(G):
                    _, _, empty, use = bank_of(("val", w, i), table)
                    act.wait_ge(empty, use)
                    act.copy(val_hi[w][:, i, 0:H], val[w][:, i, :]).then_inc(val_hi_ready, 1)

            def centre(n, g, buf, z_buf):
                act.wait_ge(inv_ready[n], g + 1)
                for i in range(G):
                    z = act.activation(z_buf[:, i, 0:H], buf[:, i, 0:H], ACT.Identity, scale=inv[n][:, 3, i:i + 1],
                                       bias=inv[n][:, 2, i:i + 1])
                z.then_inc(z_ready[n], 1)

            for i in range(G):
                divided = act.activation(tail_c[:, i, 0:H], tail_c[:, i, 0:H], ACT.Copy, scale=tail_rsum[:, 1, i:i + 1])
            divided.then_inc(tail_divided, 1)

            def iteration(t, a, n, f, o):
                table = jobs(t, a, n)
                if a:
                    bank, full, empty, use = bank_of(("u", 0), table)
                    act.wait_ge(bias_ready, t + 1)
                    for i in range(G):
                        ex = act.activation(e[:, i, :], bank[:, i * S:(i + 1) * S], ACT.Exp, scale=SCALE,
                                            bias=neg_max[:, 1, i:i + 1], accum_out=z_sum[:, i:i + 1])
                    ex.then_inc(empty, 1)
                    values_high(LEFT, t, table)
                if f:
                    if not isinstance(t, int) or t >= 2:
                        act.wait_ge(out_ready, t - 1)
                    centre(END, t - 1, c, zc)
                if a:
                    _, _, empty, use = bank_of(("et", 0), table)
                    act.wait_ge(empty, use)
                    act.copy(et_hi[:], et[:]).then_inc(et_hi_ready, 1)
                    values_high(RIGHT, t, table)
                if n:
                    centre(FRONT, t, xin, xin)
                    for k in range(KC):
                        bank, full, empty, use = bank_of(("ht", k), table)
                        act.wait_ge(full, use)
                        act.activation(ht_hi[:, k, :], bank[:], ACT.Relu)
                        act.activation(ht[:, k, :], bank[:], ACT.Relu).then_inc(empty, 1)

            run(act, iteration)

        @block.vector
        def _(dve):
            def moments(n, g, src):
                for i in range(G):
                    bn = dve.bn_stats(stats[n][:, i, :], src[:, i, 0:H])
                bn.then_inc(bn_ready[n], 1)
                dve.wait_ge(consts_set, 1)
                dve.wait_ge(bn_ready[n], g + 1)
                for i in range(G):
                    ag = dve.bn_aggr(mv[n][:, i, :], stats[n][:, i, :])
                ag.then_inc(mv_ready[n], 1)

            def values_out(w, t, table):
                for i in range(G):
                    bank, full, empty, use = bank_of(("val", w, i), table)
                    dve.wait_ge(full, use)
                    if w == SELF:
                        dve.tensor_tensor(own[:, i, 0:H], bank[:, 0:H], bias[:, w, :], ALU.add).then_inc(empty, 1)
                    else:
                        dve.tensor_tensor(val[w][:, i, :], bank[:, 0:H], bias[:, w, :], ALU.add).then_inc(empty, 1)

            dve.memset(own[:, :, H:HV], 1.0)
            for w in (LEFT, RIGHT):
                dve.memset(val_hi[w][:, :, H:H + 1].bitcast(F32), 1.0)
                dve.memset(val_hi[w][:, :, H + 1:HV].bitcast(F32), 0.0)
                last = dve.memset(val_lo[w][:, :, H:HV].bitcast(F32), 0.0)
            last.then_inc(consts_set, 1)

            def iteration(t, a, n, f, o):
                table = jobs(t, a, n)
                drain = is_step(t, groups)
                end = is_step(t, groups + 1)
                if a:
                    bank, full, _, use = bank_of(("u", 0), table)
                    dve.wait_ge(full, use)
                    dve.tensor_reduce(neg_max[:, 0, :], bank[:].rearrange("p (b j) -> p b j", b=G), AX_X, ALU.max,
                                      negate=True).then_inc(max_ready, 1)
                    dve.wait_ge(max_ready, t + 1)
                    dve.tensor_scalar(neg_max[:, 1, :], neg_max[:, 0, :], SCALE, None,
                                      ALU.mult).then_inc(bias_ready, 1)
                if f and drain:
                    moments(END, t - 1, c)
                if o:
                    if end:
                        affine(dve, t - 1)
                    dve.wait_ge(shifted, t - 1)
                    dve.wait_ge(xres_loaded, 16 * (t - 1))
                    dve.scalar_tensor_tensor(xres[:], zc[:], 0.0, xres[:], ALU.max, ALU.add).then_inc(out_ready, 1)
                if f and not drain:
                    moments(END, t - 1, c)
                if a:
                    values_out(LEFT, t, table)
                if n:
                    dve.wait_ge(x_loaded, 16 * (t + 1))
                    moments(FRONT, t, xin)
                if a:
                    bank, full, empty, use = bank_of(("et", 0), table)
                    dve.wait_ge(full, use)
                    dve.wait_ge(masks_ready, t + 1)
                    turned = bank[:].rearrange("p (b i) -> p b i", b=G)
                    dve.tensor_tensor(et[:, LEFT], turned, m_lr[:, LEFT], ALU.mult)
                    dve.tensor_tensor(et[:, RIGHT], turned, m_lr[:, RIGHT], ALU.mult).then_inc(empty, 1)
                    dve.wait_ge(diag_masked, t + 1)
                    dve.tensor_reduce(diag[:], e_diag[:], AX_X, ALU.add).then_inc(diag_ready, 1)
                    values_out(RIGHT, t, table)
                    dve.wait_ge(et_hi_ready, t + 1)
                    dve.tensor_tensor(et_lo[:], et[:], et_hi[:].bitcast(F32), ALU.subtract).then_inc(et_lo_ready, 1)
                if is_step(t, 0):
                    dve.wait_ge(tail_divided, 1)
                    moments(TAIL, 0, tail_c)
                if a:
                    values_out(SELF, t, table)
                if is_step(t, 0):
                    dve.wait_ge(inv_ready[TAIL], 1)
                    for i in range(G):
                        z = dve.tensor_scalar(tail_c[:, i, 0:H], tail_c[:, i, 0:H], mv[TAIL][:, i, 0:1],
                                              inv[TAIL][:, 3, i:i + 1], ALU.subtract, ALU.mult)
                    z.then_inc(tail_centred, 1)
                if n:
                    for k in range(KC):
                        _, _, empty, use = bank_of(("ht", k), table)
                        dve.wait_ge(empty, use)
                        dve.tensor_tensor(ht_lo[:, k, :], ht[:, k, :], ht_hi[:, k, :].bitcast(F32),
                                          ALU.subtract).then_inc(ht_ready, 1)
                if a:
                    if not isinstance(t, int) or t >= 1:
                        dve.wait_ge(z_ready[END], t)
                    dve.wait_ge(diag_ready, t + 1)
                    _, _, own_landed, own_use = bank_of(("val", SELF, G - 1), table)
                    dve.wait_ge(own_landed, own_use)
                    for i in range(G):
                        bank, full, empty, use = bank_of(("ctx", i), table)
                        dve.wait_ge(full, use)
                        dve.scalar_tensor_tensor(c[:, i, 0:H + 1], own[:, i, 0:H + 1], diag[:, i:i + 1],
                                                 bank[:, 0:H + 1], ALU.mult, ALU.add).then_inc(empty, 1)
                    dve.wait_ge(empty, use)
                    dve.scalar_tensor_tensor(q[:, 0, :], z_sum[:], SUM_EPS, c[:, :, H], ALU.mult,
                                             ALU.add).then_inc(q_ready, 1)
                if is_step(t, 1):
                    dve.wait_ge(tail_shifted, 1)
                    dve.wait_ge(tail_loaded, 16)
                    dve.scalar_tensor_tensor(tail_x[:], tail_c[:, :, 0:H], 0.0, tail_x[:], ALU.max,
                                             ALU.add).then_inc(tail_ready, 1)

            run(dve, iteration)

        @block.gpsimd
        def _(pool):
            pool.wait_ge(consts_set, 1)

            def inverse(n, step0):
                pool.tensor_tensor(inv[n][:, 3, :], inv[n][:, 0, :], num[:, RSQRT, :],
                                   ALU.pow).then_inc(inv_step[n], 1)
                pool.wait_ge(inv_step[n], step0 + 1)
                pool.tensor_tensor(inv[n][:, 1, :], inv[n][:, 3, :], mv[n][:, :, 0],
                                   ALU.mult).then_inc(inv_step[n], 1)
                pool.wait_ge(inv_step[n], step0 + 2)
                pool.tensor_tensor(inv[n][:, 2, :], inv[n][:, 1, :], num[:, MINUS_ONE, :],
                                   ALU.mult).then_inc(inv_ready[n], 1)

            def front_inverse(g):
                pool.wait_ge(mv_ready[FRONT], g + 1)
                pool.tensor_tensor(inv[FRONT][:, 0, :], mv[FRONT][:, :, 1], num[:, N_LN_EPS, :],
                                   ALU.add).then_inc(inv_step[FRONT], 1)
                pool.wait_ge(inv_step[FRONT], 3 * g + 1)
                inverse(FRONT, 3 * g + 1)

            def end_inverse(g):
                pool.wait_ge(mv_ready[END], g + 1)
                pool.wait_ge(q_ready, g + 1)
                pool.tensor_tensor(q[:, 1, :], q[:, 0, :], q[:, 0, :], ALU.mult).then_inc(inv_step[END], 1)
                pool.wait_ge(inv_step[END], 5 * g + 1)
                pool.tensor_tensor(q[:, 2, :], q[:, 1, :], num[:, N_L1_EPS, :], ALU.mult).then_inc(inv_step[END], 1)
                pool.wait_ge(inv_step[END], 5 * g + 2)
                pool.tensor_tensor(inv[END][:, 0, :], q[:, 2, :], mv[END][:, :, 1],
                                   ALU.add).then_inc(inv_step[END], 1)
                pool.wait_ge(inv_step[END], 5 * g + 3)
                inverse(END, 5 * g + 3)

            def tail_inverse():
                v, done = inv[TAIL], inv_step[TAIL]
                pool.wait_ge(mv_ready[TAIL], 1)
                pool.tensor_tensor(v[:, 0, :], mv[TAIL][:, :, 1], num[:, N_UNBIAS, :], ALU.mult).then_inc(done, 1)
                pool.wait_ge(done, 1)
                pool.tensor_tensor(v[:, 1, :], v[:, 0, :], num[:, SQRT, :], ALU.pow).then_inc(done, 1)
                pool.wait_ge(done, 2)
                pool.tensor_tensor(v[:, 2, :], v[:, 1, :], num[:, N_L0_EPS, :], ALU.add).then_inc(done, 1)
                pool.wait_ge(done, 3)
                pool.tensor_tensor(v[:, 3, :], v[:, 2, :], num[:, MINUS_ONE, :], ALU.pow).then_inc(inv_ready[TAIL], 1)

            def tail_affine():
                pool.wait_ge(tail_centred, 1)
                pool.tensor_tensor(tail_c[:, :, 0:H], tail_c[:, :, 0:H], a1[:, None, :].to_broadcast([P, G, H]),
                                   ALU.mult).then_inc(tail_scaled, 1)
                pool.wait_ge(tail_scaled, 1)
                pool.tensor_tensor(tail_c[:, :, 0:H], tail_c[:, :, 0:H], b1[:, None, :].to_broadcast([P, G, H]),
                                   ALU.add).then_inc(tail_shifted, 1)

            def values_low(w, t):
                for i in range(G):
                    pool.wait_ge(val_hi_ready, 2 * G * t + G * w + i + 1)
                    pool.tensor_tensor(val_lo[w][:, i, 0:H], val[w][:, i, :], val_hi[w][:, i, 0:H].bitcast(F32),
                                       ALU.subtract).then_inc(val_lo_ready, 1)

            def iteration(t, a, n, f, o):
                table = jobs(t, a, n)
                if a:
                    pool.wait_ge(adj_loaded, 16 * (t + 1))
                    pool.tensor_tensor(m_self[:], adj_tr[:], ident[:, None, :].to_broadcast([P, G, S]), ALU.mult)
                    for w, sign in ((LEFT, 1), (RIGHT, -1)):
                        sel = pool.affine_select(out=m_lr[:, w], in_=adj_tr[:], compare_op=ALU.is_gt, fill=0.0,
                                                 base=0, pattern=[[0, G], [-sign, S]], channel_multiplier=sign)
                    sel.then_inc(masks_ready, 1)
                if f:
                    end_inverse(t - 1)
                if a:
                    _, _, empty, use = bank_of(("u", 0), table)
                    pool.wait_ge(empty, use)
                    pool.wait_ge(masks_ready, t + 1)
                    pool.tensor_tensor(e_diag[:], e[:], m_self[:], ALU.mult).then_inc(diag_masked, 1)
                    values_low(LEFT, t)
                if n:
                    front_inverse(t)
                if a:
                    values_low(RIGHT, t)
                if is_step(t, 0):
                    tail_inverse()
                    tail_affine()
                if f and not is_step(t, groups):
                    affine(pool, t)

            run(pool, iteration)


def build(nc, x, adj, adj_t, l0_w_left, l0_w_right, l0_w_lin_t, l0_b_lin, l0_ln_cols, l0_ln_a1, l0_ln_b1,
          l1_w_left_t, l1_w_self_t, l1_w_right_t, l1_biases, l1_gamma, l1_beta, out):
    H = x.shape[2]
    KC, GS = H // P, G * P
    x2 = nc.dram_tensor("x2_scratch", list(x.shape), F32, kind="Internal").ap()
    with ExitStack() as ctx:
        def sb(name, shape, dt=F32):
            return ctx.enter_context(nc.sbuf_tensor(name, shape, dt))

        kept = {
            "w_hi": [sb(f"kept_w_hi{w}", [P, KC, H], F32R) for w in range(3)],
            "w_lo": [sb(f"kept_w_lo{w}", [P, KC, H], F32R) for w in range(3)],
            "x2_stored": ctx.enter_context(nc.semaphore("x2_stored")),
            "ident": sb("ident", [P, P]),
            "num": sb("num", [P, N_L1_EPS + 1, G]),
            "xin": sb("xin", [P, G, H]),
            "xres": sb("xres", [P, G, H]),
            "c": sb("c_b", [P, G, H + 2]),
            "rsum": sb("rsum_b", [P, 2, G]),
            "a1": sb("a1", [P, H]),
            "b1": sb("b1", [P, H]),
            "ht": sb("ht", [P, KC, GS]),
            "ht_hi": sb("ht_hi", [P, KC, GS], F32R),
            "ht_lo": sb("ht_lo", [P, KC, GS], F32R),
            "l1_consts": [sb("l1_bias", [P, 3, H]), sb("l1_gamma", [P, H]), sb("l1_beta", [P, H])],
        }
        l0_phase(nc, kept, x, adj, adj_t, l0_w_left, l0_w_right, l0_w_lin_t, l0_b_lin, l0_ln_cols, l0_ln_a1,
                 l0_ln_b1, (l1_biases, l1_gamma, l1_beta), (l1_w_left_t, l1_w_right_t, l1_w_self_t), x2)
        l1_phase(nc, kept, x, x2, adj_t, out)


def kernel(**inputs):
    import numpy as np
    import concourse.bacc as bacc
    from concourse.bass_utils import run_bass_kernel_spmd

    i = {k: np.asarray(v) for k, v in inputs.items()}
    chunks = i["x"].shape[2] // P
    laid = {
        "x": i["x"],
        "adj": i["adj"],
        "adj_t": i["adj"].transpose(0, 2, 1),
        "l0_w_left": i["L0_gnn_W_left"],
        "l0_w_right": i["L0_gnn_W_right"],
        "l0_w_lin_t": i["L0_gnn_W_lin"].transpose(0, 2, 1),
        "l0_b_lin": i["L0_gnn_b_lin"],
        "l0_ln_cols": np.stack([i["L0_gnn_ln_a"][0].reshape(chunks, P).T, i["L0_gnn_ln_b"][0].reshape(chunks, P).T], 1),
        "l0_ln_a1": i["L0_gnn_ln_a"][1],
        "l0_ln_b1": i["L0_gnn_ln_b"][1],
        "l1_w_left_t": i["L1_gnn_W_left"].T,
        "l1_w_self_t": i["L1_gnn_W_self"].T,
        "l1_w_right_t": i["L1_gnn_W_right"].T,
        "l1_biases": np.stack([i["L1_gnn_b_left"], i["L1_gnn_b_right"], i["L1_gnn_b_self"]]),
        "l1_gamma": i["L1_gnn_gamma"],
        "l1_beta": i["L1_gnn_beta"],
    }
    nc = bacc.Bacc("TRN2", target_bir_lowering=False, num_devices=1)
    arrays, args = {}, []
    for name, a in laid.items():
        a = np.ascontiguousarray(a)
        arrays[f"in_{name}"] = a
        args.append(nc.dram_tensor(f"in_{name}", a.shape, mybir.dt.from_np(a.dtype), kind="ExternalInput").ap())
    args.append(nc.dram_tensor("out_0", i["x"].shape, mybir.dt.from_np(i["x"].dtype), kind="ExternalOutput").ap())
    build(nc, *args)
    r = run_bass_kernel_spmd(nc, [arrays], core_ids=[0])
    return r.results[0]["out_0"]
```
